# Optimizing a Trainium2 kernel written in Bass

```python
import numpy as np
import jax
import jax.numpy as jnp

def _softmax(x, axis=-1):
    return jax.nn.softmax(x, axis=axis)

def _gelu(x):
    return jax.nn.gelu(x, approximate=True)

def _silu(x):
    return jax.nn.silu(x)

def _sigmoid(x):
    return jax.nn.sigmoid(x)

def _layernorm(x, axis=-1, eps=1e-05):
    m = jnp.mean(x, axis=axis, keepdims=True)
    v = jnp.var(x, axis=axis, keepdims=True)
    return (x - m) / jnp.sqrt(v + eps)

def _scatter_add(tgt, idx, src, axis=0):
    return tgt.at[idx].add(src)

def _segment_sum(src, seg, n):
    return jax.ops.segment_sum(src, seg, n)
kernel_name = 'mk_gnn_preln_d1_gnn_r8_ca77dd'

def setup_inputs(seed: int=0):
    np.random.seed(seed)
    _w = jnp.asarray

    def _rec_inputs():
        import jax
        import jax.numpy as jnp
        _gk = jax.random.key(seed)
        x = -0.000202 + 1 * jax.random.normal(jax.random.fold_in(_gk, 1), (6250, 128), jnp.float32)
        src = jax.random.randint(jax.random.fold_in(_gk, 2), (200000,), 0, 6250, jnp.int32)
        dst = jnp.minimum((6250 * jax.random.uniform(jax.random.fold_in(_gk, 3), (200000,)) ** 2.0).astype(jnp.int32), 49999)
        _o = jnp.argsort(dst, stable=True)
        src = src[_o]
        dst = dst[_o]
        edge_attr_20 = jax.random.uniform(jax.random.fold_in(_gk, 11), (200000, 20), jnp.float32, 0.0, 1)
        edge_weight1 = jax.random.uniform(jax.random.fold_in(_gk, 13), (200000, 1), jnp.float32, 0.0, 1)
        return (x, src, dst, edge_attr_20, edge_weight1)
    x, src, dst, edge_attr_20, edge_weight1 = _rec_inputs()

    def _L0_gnn_setup():
        import jax, jax.numpy as jnp
        import numpy as np
        N_ATOMS = 6250
        N_PAIRS = 200000
        F = 128
        NF = 128
        RBF = 20
        LOG2 = float(np.log(2.0))

        def shifted_softplus(x):
            return jax.nn.softplus(x) - LOG2
        key = jax.random.key(seed)
        ks = jax.random.split(key, 12)
        inv = lambda n: 1.0 / np.sqrt(n)
        return {'atomic_embedding': jax.random.normal(ks[0], (N_ATOMS, F), jnp.float32), 'pair_indices': jax.random.randint(ks[1], (2, N_PAIRS), 0, N_ATOMS, jnp.int32), 'f_ij': jax.random.uniform(ks[2], (N_PAIRS, RBF), jnp.float32), 'f_ij_cutoff': jax.random.uniform(ks[3], (N_PAIRS, 1), jnp.float32), 'W_in': jax.random.normal(ks[4], (F, NF), jnp.float32) * inv(F), 'W_f1': jax.random.normal(ks[5], (RBF, NF), jnp.float32) * inv(RBF), 'b_f1': jnp.zeros((NF,), jnp.float32), 'W_f2': jax.random.normal(ks[6], (NF, NF), jnp.float32) * inv(NF), 'b_f2': jnp.zeros((NF,), jnp.float32), 'W_o1': jax.random.normal(ks[7], (NF, F), jnp.float32) * inv(NF), 'b_o1': jnp.zeros((F,), jnp.float32), 'W_o2': jax.random.normal(ks[8], (F, F), jnp.float32) * inv(F), 'b_o2': jnp.zeros((F,), jnp.float32)}
    _L0_gnn_all = _L0_gnn_setup()
    _L0_gnn_in = {k: v for k, v in _L0_gnn_all.items() if k in ('W_in', 'W_f1', 'b_f1', 'W_f2', 'b_f2', 'W_o1', 'b_o1', 'W_o2', 'b_o2')}
    del _L0_gnn_all
    return {'x': x, 'src': src, 'dst': dst, 'edge_attr_20': edge_attr_20, 'edge_weight1': edge_weight1, 'L0_gnn_W_in': _L0_gnn_in['W_in'], 'L0_gnn_W_f1': _L0_gnn_in['W_f1'], 'L0_gnn_b_f1': _L0_gnn_in['b_f1'], 'L0_gnn_W_f2': _L0_gnn_in['W_f2'], 'L0_gnn_b_f2': _L0_gnn_in['b_f2'], 'L0_gnn_W_o1': _L0_gnn_in['W_o1'], 'L0_gnn_b_o1': _L0_gnn_in['b_o1'], 'L0_gnn_W_o2': _L0_gnn_in['W_o2'], 'L0_gnn_b_o2': _L0_gnn_in['b_o2']}

def reference(x, src, dst, edge_attr_20, edge_weight1, L0_gnn_W_in, L0_gnn_W_f1, L0_gnn_b_f1, L0_gnn_W_f2, L0_gnn_b_f2, L0_gnn_W_o1, L0_gnn_b_o1, L0_gnn_W_o2, L0_gnn_b_o2):
    import jax
    import jax.numpy as jnp

    def _L0_gnn_ref(atomic_embedding, pair_indices, f_ij, f_ij_cutoff, W_in, W_f1, b_f1, W_f2, b_f2, W_o1, b_o1, W_o2, b_o2):
        import jax, jax.numpy as jnp
        import numpy as np
        N_ATOMS = 6250
        N_PAIRS = 200000
        F = 128
        NF = 128
        RBF = 20
        LOG2 = float(np.log(2.0))

        def shifted_softplus(x):
            return jax.nn.softplus(x) - LOG2
        idx_i = pair_indices[0]
        idx_j = pair_indices[1]
        x = atomic_embedding @ W_in
        W_ij = shifted_softplus(f_ij @ W_f1 + b_f1) @ W_f2 + b_f2
        W_ij = W_ij * f_ij_cutoff
        x_ij = x[idx_j] * W_ij
        out = jax.ops.segment_sum(x_ij, idx_i, num_segments=N_ATOMS)
        return shifted_softplus(out @ W_o1 + b_o1) @ W_o2 + b_o2
    edge_index = jnp.stack([src, dst])
    h = jnp.maximum(_layernorm(x, axis=-1), 0.0)
    x = x + _L0_gnn_ref(h, edge_index, edge_attr_20, edge_weight1, L0_gnn_W_in, L0_gnn_W_f1, L0_gnn_b_f1, L0_gnn_W_f2, L0_gnn_b_f2, L0_gnn_W_o1, L0_gnn_b_o1, L0_gnn_W_o2, L0_gnn_b_o2)
    return x

_drawn_inputs = setup_inputs


def setup_inputs(seed=0):
    import zlib

    import numpy as np

    out = dict(_drawn_inputs(seed))
    spreads = {'L0_gnn_b_f1': (0.0, 0.1),
     'L0_gnn_b_f2': (0.0, 0.1),
     'L0_gnn_b_o1': (0.0, 0.1),
     'L0_gnn_b_o2': (0.0, 0.1)}
    factors = {}
    for name, (base, spread) in spreads.items():
        noise = np.random.default_rng([zlib.crc32(name.encode()), seed]).standard_normal(out[name].shape)
        drawn = base * np.exp(spread * noise) if base else spread * noise
        out[name] = jnp.asarray(drawn.astype(out[name].dtype))
    for name, factor in factors.items():
        out[name] = (out[name] * factor).astype(out[name].dtype)
    return out
```

```python
from contextlib import ExitStack
import math

import concourse.bass as bass
from concourse import mybir

P = 128
T = 4
CE = P * T
LAST_PEELED = 6
UNROLL = 4


def gnn_kernel(nc, x, src, dst, edge_attr, cutoff, W_in, W_f1, b_f1, W_f2, b_f2, W_o1, b_o1, W_o2, b_o2, out):
    fp32, bf16, i32, i16 = mybir.dt.float32, mybir.dt.bfloat16, mybir.dt.int32, mybir.dt.int16
    ALU, ACT, AX = mybir.AluOpType, mybir.ActivationFunctionType, mybir.AxisListType

    N, F = x.shape
    E, RBF = edge_attr.shape
    NCH = -(-E // CE)
    TAIL = E - CE
    REPEATED = (NCH - 1) * CE - TAIL
    assert N % P == 0 or -(-N // P) % 4 == 1
    assert REPEATED % T == 0 and REPEATED // T in (0, 32, 48, 64, 96) and F == P
    G = -(-NCH // P)
    rows_of = [min(P, NCH - g * P) for g in range(G)]
    NB = -(-N // P)
    NLAST = N - (NB - 1) * P
    NQ = -(-NB // 4)
    ACC_ROWS = -(-(N + P) // (10 * P)) * 10 * P
    LN2 = math.log(2.0)

    acc = [nc.dram_tensor(f"acc{t}", (ACC_ROWS, F), fp32, kind="Internal").ap() for t in range(T)]
    xw_parts = nc.dram_tensor("xw_parts", (N, 3 * F), bf16, kind="Internal").ap()
    src_rows = nc.dram_tensor("src_rows", (NCH, CE), i16, kind="Internal").ap()
    dst_rows = nc.dram_tensor("dst_rows", (NCH, CE), i16, kind="Internal").ap()

    ctx = ExitStack()
    with ctx:
        def sb(name, shape, dt=fp32):
            return ctx.enter_context(nc.sbuf_tensor(name, shape, dt))

        def pb(name, shape, dt=fp32):
            return ctx.enter_context(nc.psum_tensor(name, shape, dt))

        def sem(name):
            return ctx.enter_context(nc.semaphore(name))

        ident = sb("ident", [P, P])
        ones = sb("ones", [P, P])
        ones_bf = sb("ones_bf", [P, P], bf16)
        column_no = sb("column_no", [P, P])
        row_no = sb("row_no", [P, 1])
        is_row = sb("is_row", [P, 3])
        earlier = sb("earlier", [P, P])
        spare_row = sb("spare_row", [P, 1])
        w_in = sb("w_in", [P, F])
        KA = T * RBF
        w_f1 = sb("w_f1", [KA + 1, T, F])
        w_f2 = sb("w_f2", [P, F])
        w_o1 = sb("w_o1", [P, F])
        w_o2 = sb("w_o2", [P, F])
        bo1 = sb("bo1", [P, 1])
        bf2_row = sb("bf2_row", [P, F])
        bo2_row = sb("bo2_row", [P, F])
        bf2_hi = sb("bf2_hi", [P, F], bf16)
        bf2_mid = sb("bf2_mid", [P, F], bf16)
        bf2_rest = sb("bf2_rest", [P, F])
        bf2_sum = sb("bf2_sum", [P, F])
        bf2_parts = sb("bf2_parts", [P, T, F], bf16)
        ZB = 10
        assert ACC_ROWS // P % ZB == 0
        zeros = sb("zeros", [P, ZB * F])
        xs = sb("xs", [P, NB, F])
        stats = sb("stats", [P, NB, 6])
        meanvar = sb("meanvar", [P, NB, 2])
        std = sb("std", [P, NB])
        rstd = sb("rstd", [P, NB])
        EB = 8
        NPC = -(-NB // EB)
        shared_a = sb("shared_a", [P, max(NB * F, 2 * T * EB * F, 14 * CE)])
        shared_b = sb("shared_b", [P, max(3 * G * CE, 3 * 2 * EB * F)])
        shared_c = sb("shared_c", [P, max(2 * G * CE, 2 * 2 * EB * F)])
        normed = shared_a[:, 0:NB * F].rearrange("p (b f) -> p b f", f=F)
        hT = sb("hT", [P, 2, 4 * P])
        shared_d = sb("shared_d", [P, 4 * T * 3 * F], bf16)
        parts = shared_d[:, 0:2 * 4 * 3 * F].rearrange("p (h b k f) -> p h b k f", h=2, b=4, k=3)
        rest = shared_d[:, 2 * 4 * 3 * F:2 * 4 * 5 * F].bitcast(fp32).rearrange("p (h n) -> p h n", h=2)
        gathered = shared_d[:, :].rearrange("p (s t c) -> p s t c", s=4, t=T)
        chunk_i = shared_c[:, 0:2 * G * CE].bitcast(i32).rearrange("p (k g e) -> p k g e", k=2, g=G)
        chunk_f = shared_b[:, 0:3 * G * CE].rearrange("p (k g e) -> p k g e", k=3, g=G)
        shared_e = sb("shared_e", [P, max(G * CE, 2 * EB * F)])
        chunk_16 = shared_e[:, 0:G * CE].bitcast(i16).rearrange("p (k g e) -> p k g e", k=2, g=G)
        dst_min = sb("dst_min", [P, G])
        dst_max = sb("dst_max", [P, G])
        spread = sb("spread", [P, G])
        diag = sb("diag", [P, G, 2, P])
        src_col = sb("src_col", [P, G * P, T])
        src_less_spare = sb("src_less_spare", [P, G * P, T])
        cut_col = sb("cut_col", [P, G * P, T])
        dst_col = sb("dst_col", [P, G * P, T], i32)
        window_col = sb("window_col", [P, G * P])
        base_row = sb("base_row", [1, G * P], i32)
        spread_row = sb("spread_row", [1, G * P])
        far = sb("far", [1, 1])
        in_order = sb("in_order", [1, 1], i32)
        attr = sb("attr", [P, 4, T * RBF])
        dst_b = sb("dst_b", [P, 4, CE], i16)
        src_b = sb("src_b", [P, 4, CE], i16)
        xwin = sb("xwin", [P, 4, 3 * F], bf16)
        dst_now = sb("dst_now", [P, 4, T], i32)
        attrT = sb("attrT", [96, 2, P])
        onehot = sb("onehot", [P, 2, CE], bf16)
        same_earlier = sb("same_earlier", [P, 2, CE], bf16)
        n_earlier = sb("n_earlier", [P, 4, T])
        picked = sb("picked", [P, 4, T])
        target = sb("target", [P, 4, T], i32)
        hidden_exp, hidden, xg, message, same = (
            shared_a[:, k * 2 * CE:(k + 1) * 2 * CE].rearrange("p (h e) -> p h e", h=2) for k in range(5))
        summed = shared_a[:, 10 * CE:14 * CE].rearrange("p (s e) -> p s e", s=4)
        acc_sb = shared_a[:, 0:2 * T * EB * F].rearrange("p (h t b f) -> p h t b f", h=2, t=T, b=EB)
        total = shared_b[:, 0:2 * EB * F].rearrange("p (h b f) -> p h b f", h=2, b=EB)
        totalT, size_o = (shared_b[:, k * 2 * EB * F:(k + 1) * 2 * EB * F].rearrange("p (h n) -> p h n", h=2) for k in (1, 2))
        relu_o, hid_o = (shared_c[:, k * 2 * EB * F:(k + 1) * 2 * EB * F].rearrange("p (h n) -> p h n", h=2) for k in (0, 1))
        out_sb = shared_e[:, 0:2 * EB * F].rearrange("p (h b f) -> p h b f", h=2, b=EB)

        ps = [pb(f"ps{i}", [P, 512]) for i in range(8)]
        attrT_ps, hidden_ps = ps[0], ps[1]
        filter_ps, xg_ps, summed_ps = ps[2:4], ps[4:6], ps[6:8]

        s_xs = sem("x_loaded")
        s_w = sem("weights_loaded")
        s_chunks = [sem("src_loaded"), sem("dst_loaded"), sem("cutoff_loaded")]
        s_iota = sem("iota_done")
        s_const = sem("constants_ready")
        s_w1z = sem("w_f1_cleared")
        s_zero = sem("zeros_ready")
        s_accz = sem("accumulators_cleared")
        s_var = sem("variance_ready")
        s_std = sem("std_ready")
        s_chain = sem("dve_chain")
        s_norm = sem("normed_ready")
        s_tr = sem("hT_in_psum")
        s_hT = sem("hT_ready")
        s_xw = sem("xw_in_psum")
        s_hi = sem("xw_hi_ready")
        s_rest = sem("xw_rest_ready")
        s_mid = sem("xw_mid_ready")
        s_lo = sem("xw_lo_ready")
        s_parts = [sem("xw_parts_stored_even"), sem("xw_parts_stored_odd")]
        s_bias = sem("bias_sums_in_psum")
        s_biasr = sem("bias_rows_ready")
        s_ch16 = sem("chunk_rows_16_ready")
        s_rows = sem("chunk_rows_stored")
        s_chf = sem("chunk_rows_float_ready")
        s_colps = sem("columns_in_psum")
        s_col = sem("columns_ready")
        s_diag = sem("diagonals_ready")
        s_bps = sem("bases_in_psum")
        s_base = sem("bases_ready")
        s_flag = sem("order_flag_ready")
        s_attr = [sem(f"attr_loaded{k}") for k in range(4)]
        s_dstb = [sem(f"dst_loaded{k}") for k in range(4)]
        s_srcb = [sem(f"src_loaded{k}") for k in range(4)]
        s_xwin = [sem(f"window_loaded{k}") for k in range(4)]
        s_gath = [sem(f"rows_gathered{k}") for k in range(4)]
        s_scat = [sem(f"scattered{t}") for t in range(T)]
        s_aTp = sem("attrT_in_psum")
        s_aT = sem("attrT_ready")
        s_hp = sem("hidden_in_psum")
        s_size = sem("hidden_size_ready")
        s_exp = sem("hidden_exp_ready")
        s_log = sem("hidden_log_ready")
        s_h = sem("hidden_ready")
        s_ones = sem("attrT_ones_ready")
        s_oh = sem("onehot_ready")
        s_dnow = sem("dst_now_ready")
        s_same = sem("same_ready")
        s_first = sem("n_earlier_ready")
        s_go = sem("pool_may_go")
        s_sp_go = sem("sync_may_go")
        s_pick = sem("picked_ready")
        s_idx = sem("targets_ready")
        s_xgp = sem("xg_in_psum")
        s_xg = sem("xg_ready")
        s_fp = sem("filter_in_psum")
        s_msg = sem("message_ready")
        s_sp = sem("sums_in_psum")
        s_s = sem("sums_ready")
        s_ald = [sem("acc_loaded_even"), sem("acc_loaded_odd")]
        s_add = sem("acc_added")
        s_tp = sem("totalT_in_psum")
        s_t = sem("totalT_ready")
        s_o1 = sem("out_hidden_in_psum")
        s_so = sem("out_size_ready")
        s_eo = sem("out_exp_ready")
        s_lo1 = sem("out_log_and_relu_ready")
        s_o1s = sem("out_hidden_ready")
        s_o2 = sem("out_in_psum")
        s_o = sem("out_ready")
        s_ost = [sem("out_stored_even"), sem("out_stored_odd")]
        s_res = sem("residual_ready")

        def quad(q):
            b = range(4 * q, min(4 * q + 4, NB))
            return b, (NLAST if b[-1] == NB - 1 and NLAST < P else P)

        def piece(q):
            return range(EB * q, min(EB * q + EB, NB))

        def stores_until(q_end, h):
            n = 0
            for q in range(h, q_end, 2):
                b = piece(q)
                ragged = b[-1] == NB - 1 and NLAST < P
                n += 2 if ragged and len(b) > 1 else 1
            return n

        ndma = sum(1 for g in range(G) if min(rows_of[g], NCH - 1 - g * P) > 0) + 1
        o2_count = sum(-(-len(piece(q)) * P // 512) for q in range(NPC))

        def steps(eng, step):
            turns = max(0, (NCH - 2 - LAST_PEELED) // UNROLL)
            for i in range(-2, LAST_PEELED):
                step(i, i % 4)
            if turns:
                with eng.Fori(0, turns) as turn:
                    for j in range(UNROLL):
                        step(turn * UNROLL + (LAST_PEELED + j), (LAST_PEELED + j) % 4)
            for i in range(LAST_PEELED + turns * UNROLL, NCH + 1):
                step(i, i % 4)

        def known(c):
            return type(c) is int

        def exists(c):
            return not known(c) or 0 <= c < NCH

        def after(eng, semaphore, c, per=1):
            if not known(c) or c >= 0:
                eng.wait_ge(semaphore, c * per + per)

        def after_slot(eng, semaphores, c, slot, dmas=1):
            if not known(c) or c >= 0:
                eng.wait_ge(semaphores[slot], (c - slot) * (4 * dmas) + 16 * dmas)

        def both_orders(eng, value_of, body):
            eng.wait_ge(s_flag, 1)
            flag = value_of()
            with eng.If(flag == 1):
                body(True)
            with eng.Else():
                body(False)

        block = ctx.enter_context(nc.Block())

        @block.sync
        def _(sp):
            full = NCH - 1
            for k, a in enumerate((dst, src)):
                for g in range(G):
                    r = min(rows_of[g], full - g * P)
                    if r > 0:
                        sp.dma_start(chunk_i[0:r, 1 - k, g, :], a[g * P * CE:(g * P + r) * CE].rearrange("(c e) -> c e", e=CE)).then_inc(s_chunks[1 - k], 16)
                r = (NCH - 1) % P
                sp.dma_start(chunk_i[r:r + 1, 1 - k, G - 1, :], a[TAIL:E].rearrange("(c e) -> c e", e=CE)).then_inc(s_chunks[1 - k], 16)
            for g in range(G):
                r = min(rows_of[g], full - g * P)
                if r > 0:
                    sp.dma_start(chunk_f[0:r, 2, g, :], cutoff[g * P * CE:(g * P + r) * CE, :].rearrange("(c e) o -> c (e o)", e=CE)).then_inc(s_chunks[2], 16)
            r = (NCH - 1) % P
            sp.dma_start(chunk_f[r:r + 1, 2, G - 1, :], cutoff[TAIL:E, :].rearrange("(c e) o -> c (e o)", e=CE)).then_inc(s_chunks[2], 16)
            sp.wait_ge(s_zero, 1)
            for t in range(T):
                sp.dma_start(acc[t].rearrange("(p k r) f -> p k (r f)", p=P, r=ZB),
                             zeros[:, :].unsqueeze(1).to_broadcast([P, ACC_ROWS // P // ZB, ZB * F])).then_inc(s_accz, 16)
            for k, a in ((1, dst_rows), (0, src_rows)):
                sp.wait_ge(s_ch16, 2 - k)
                for g in range(G):
                    sp.dma_start(a[g * P:g * P + rows_of[g], :], chunk_16[0:rows_of[g], k, g, :]).then_inc(s_rows, 16)
            for q in range(NQ):
                blocks, last = quad(q)
                sp.wait_ge(s_lo, q + 1)
                n = len(blocks) if last == P else len(blocks) - 1
                if n:
                    sp.dma_start(xw_parts[4 * q * P:(4 * q + n) * P, :].rearrange("(b p) c -> p b c", p=P),
                                 parts[:, q % 2, 0:n, :, :].rearrange("p b k f -> p b (k f)")).then_inc(s_parts[q % 2], 16)
                if last < P:
                    sp.dma_start(xw_parts[blocks[-1] * P:N, :],
                                 parts[0:last, q % 2, n, :, :].rearrange("p k f -> p (k f)")).then_inc(s_parts[q % 2], 16)
            sp.wait_ge(s_rows, 16 * 2 * G)
            parts_done = [sum(1 if (quad(q)[1] == P or len(quad(q)[0]) == 1) else 2 for q in range(h, NQ, 2)) for h in range(2)]
            for h in range(2):
                if parts_done[h]:
                    sp.wait_ge(s_parts[h], 16 * parts_done[h])

            def loads(in_order):
                def step(i, m):
                    c, slot = i + 2, (m + 2) % 4
                    if not exists(c):
                        return
                    after(sp, s_aTp, c - 4)
                    if known(c) and c == NCH - 1:
                        rows = edge_attr[TAIL:E, :]
                    else:
                        rows = edge_attr[bass.ds(c * CE, CE), :]
                    sp.dma_start(attr[:, slot, :], rows.rearrange("(p t) k -> p (t k)", t=T)).then_inc(s_attr[slot], 16)
                    after(sp, s_first, c - 4)
                    sp.sem_inc(s_sp_go, 1)
                    sp.dma_start(src_b[:, slot, :], src_rows[bass.ds(c, 1), :].to_broadcast([P, CE])).then_inc(s_srcb[slot], 16)
                    if in_order:
                        after(sp, s_oh, c - 4)
                        sp.dma_start(dst_b[:, slot, :], dst_rows[bass.ds(c, 1), :].to_broadcast([P, CE])).then_inc(s_dstb[slot], 16)
                        base = sp.value_load(base_row[0:1, bass.ds(c, 1)], min_val=0, max_val=N - P)
                        after(sp, s_xgp, c - 4)
                        sp.dma_start(xwin[:, slot, :], xw_parts[bass.ds(base, P), :]).then_inc(s_xwin[slot], 16)
                steps(sp, step)
            sp.wait_ge(s_base, 1)
            both_orders(sp, lambda: sp.value_load(in_order[0:1, 0:1], min_val=0, max_val=1), loads)

            for t in range(T):
                sp.wait_ge(s_scat[t], 16 * NCH)
            for q in range(NPC):
                b = piece(q)
                if q >= 2:
                    sp.wait_ge(s_add, q - 1)
                for t in range(T):
                    sp.dma_start(acc_sb[:, q % 2, t, 0:len(b), :],
                                 acc[t][b[0] * P:(b[-1] + 1) * P, :].rearrange("(b p) f -> p b f", p=P)).then_inc(s_ald[q % 2], 16)

        @block.gpsimd
        def _(pool):
            nc.gpsimd.iota(column_no[:, :], [[1, P]], base=0, channel_multiplier=0,
                           allow_small_or_imprecise_dtypes=True).then_inc(s_iota, 1)
            nc.gpsimd.iota(row_no[:, :], [[0, 1]], base=0, channel_multiplier=1,
                           allow_small_or_imprecise_dtypes=True).then_inc(s_iota, 1)
            nc.gpsimd.memset(w_f1[:, :, :], 0.0).then_inc(s_w1z, 1)
            nc.gpsimd.memset(zeros[:, :], 0.0).then_inc(s_zero, 1)
            pool.wait_ge(s_accz, 16 * T)
            pool.wait_ge(s_rows, 16 * 2 * G)
            for h in range(2):
                n = sum(1 if (quad(q)[1] == P or len(quad(q)[0]) == 1) else 2 for q in range(h, NQ, 2))
                if n:
                    pool.wait_ge(s_parts[h], 16 * n)

            def scatters(in_order):
                def step(i, m):
                    c, slot = i + 1, (m + 1) % 4
                    if not in_order and exists(c):
                        after(pool, s_xg, c - 4)
                        after(pool, s_dnow, c)
                        pool.sem_inc(s_go, 1)
                        for t in range(T):
                            nc.gpsimd.indirect_dma_start(
                                out=gathered[:, slot, t, :], out_offset=None, in_=xw_parts[:, :],
                                in_offset=bass.IndirectOffsetOnAxis(ap=dst_now[:, slot, t:t + 1], axis=0)).then_inc(s_gath[slot], 16)
                    c, slot = i - 1, (m - 1) % 4
                    if exists(c):
                        after(pool, s_idx, c)
                        after(pool, s_s, c)
                        for t in range(T):
                            after(pool, s_scat[t], c - 1, 16)
                            pool.sem_inc(s_go, 1)
                            nc.gpsimd.indirect_dma_start(
                                out=acc[t], out_offset=bass.IndirectOffsetOnAxis(ap=target[:, slot, t:t + 1], axis=0),
                                in_=summed[:, slot, t * F:(t + 1) * F], in_offset=None,
                                compute_op=ALU.add).then_inc(s_scat[t], 16)
                steps(pool, step)
            both_orders(pool, lambda: pool.value_load(in_order[0:1, 0:1], min_val=0, max_val=1), scatters)

            for q in range(NPC):
                b = piece(q)
                pool.wait_ge(s_o, q + 1)
                nf = len(b) if (b[-1] < NB - 1 or NLAST == P) else len(b) - 1
                if nf:
                    pool.dma_start(out[b[0] * P:(b[0] + nf) * P, :].rearrange("(b p) f -> p b f", p=P),
                                  out_sb[:, q % 2, 0:nf, :]).then_inc(s_ost[q % 2], 16)
                if nf < len(b):
                    pool.dma_start(out[b[-1] * P:N, :], out_sb[0:NLAST, q % 2, nf, :]).then_inc(s_ost[q % 2], 16)
            for h in range(2):
                pool.wait_ge(s_ost[h], 16 * stores_until(NPC, h))


        @block.scalar
        def _(act):
            nfull = NB if NLAST == P else NB - 1
            act.dma_start(xs[:, 0:nfull, :], x[0:nfull * P, :].rearrange("(b p) f -> p b f", p=P)).then_inc(s_xs, 16)
            if nfull < NB:
                act.dma_start(xs[0:NLAST, nfull, :], x[nfull * P:N, :]).then_inc(s_xs, 16)
            for tile, a in ((w_in, W_in), (w_f2, W_f2), (w_o1, W_o1), (w_o2, W_o2)):
                act.dma_start(tile[:, :], a).then_inc(s_w, 16)
            act.dma_start(bo1[:, :], b_o1.rearrange("(p o) -> p o", o=1)).then_inc(s_w, 16)
            for tile, a in ((bf2_row, b_f2), (bo2_row, b_o2)):
                act.dma_start(tile[:, :], a.rearrange("(o f) -> o f", o=1).to_broadcast([P, F])).then_inc(s_w, 16)
            act.wait_ge(s_w1z, 1)
            for t in range(T):
                act.dma_start(w_f1[t * RBF:(t + 1) * RBF, t, :], W_f1).then_inc(s_w, 16)
                act.dma_start(w_f1[KA:KA + 1, t, :], b_f1.rearrange("(o f) -> o f", o=1)).then_inc(s_w, 16)
            act.wait_ge(s_var, 1)
            nc.scalar.activation(std[:, :], std[:, :], ACT.Sqrt).then_inc(s_std, 1)
            nc.scalar.preload_act_table_set("natural_log_exp_and_others")

            def relu(q):
                blocks, last = quad(q)
                w = (len(blocks) - 1) * P + last
                act.wait_ge(s_tr, q + 1)
                if q >= 2:
                    act.wait_ge(s_xw, q - 1)
                nc.scalar.activation(hT[:, q % 2, 0:w], ps[q % 2][:, 0:w], ACT.Relu).then_inc(s_hT, 1)

            def high(q):
                blocks, last = quad(q)
                n = len(blocks)
                r = P if n > 1 else last
                act.wait_ge(s_xw, q + 1)
                if q >= 2:
                    act.wait_ge(s_parts[q % 2], 16 * sum(1 if (quad(k)[1] == P or len(quad(k)[0]) == 1) else 2 for k in range(q % 2, q - 1, 2)))
                nc.scalar.activation(parts[0:r, q % 2, 0:n, 0, :], ps[2 + q % 2][0:r, 0:n * F].rearrange("p (b f) -> p b f", f=F),
                                     ACT.Copy).then_inc(s_hi, 1)

            def middle(q):
                blocks, last = quad(q)
                n = len(blocks)
                r = P if n > 1 else last
                act.wait_ge(s_rest, q + 1)
                nc.scalar.activation(parts[0:r, q % 2, 0:n, 1, :], rest[0:r, q % 2, 0:n * F].rearrange("p (b f) -> p b f", f=F),
                                     ACT.Copy).then_inc(s_mid, 1)

            for q in range(NQ + 1):
                if q < NQ:
                    relu(q)
                if q >= 1:
                    high(q - 1)
                    middle(q - 1)

            def evacuate(in_order):
                def step(i, m):
                    c = i + 2
                    if exists(c):
                        after(act, s_aTp, c)
                        after(act, s_hp, c - 2)
                        nc.scalar.activation(attrT[0:KA, m % 2, :], attrT_ps[0:KA, m % 2 * P:m % 2 * P + P],
                                             ACT.Copy).then_inc(s_aT, 1)
                    c, odd = i + 1, (m + 1) % 2
                    if exists(c):
                        after(act, s_hp, c)
                        after(act, s_h, c - 2)
                        nc.scalar.activation(hidden_exp[:, odd, :], hidden_ps[:, :], ACT.Abs).then_inc(s_size, 1)
                        after(act, s_size, c)
                        nc.scalar.activation(hidden_exp[:, odd, :], hidden_exp[:, odd, :], ACT.Exp, scale=-1.0).then_inc(s_exp, 1)
                        after(act, s_exp, c)
                        nc.scalar.activation(hidden_exp[:, odd, :], hidden_exp[:, odd, :], ACT.Ln, bias=1.0).then_inc(s_log, 1)
                    c, odd = i, m % 2
                    if in_order and exists(c):
                        after(act, s_xgp, c)
                        after(act, s_msg, c - 2)
                        nc.scalar.activation(xg[:, odd, :], xg_ps[odd][:, :], ACT.Copy).then_inc(s_xg, 1)
                    c, odd, slot = i - 1, (m - 1) % 2, (m - 1) % 4
                    if exists(c):
                        after(act, s_sp, c)
                        for t in range(T):
                            after(act, s_scat[t], c - 4, 16)
                        nc.scalar.activation(summed[:, slot, :], summed_ps[odd][:, :], ACT.Copy).then_inc(s_s, 1)
                steps(act, step)
            act.wait_ge(s_ones, 1)
            both_orders(act, lambda: act.value_load(in_order[0:1, 0:1], min_val=0, max_val=1), evacuate)

            for q in range(NPC):
                n = len(piece(q)) * P
                for h in range(0, n, 512):
                    w = min(512, n - h)
                    k = q * (EB * P // 512) + h // 512
                    act.wait_ge(s_o1, k + 1)
                    if q >= 2:
                        act.wait_ge(s_o1s, k - 3)
                    z, a = ps[4 + h // 512][:, 0:w], size_o[:, q % 2, h:h + w]
                    nc.scalar.activation(relu_o[:, q % 2, h:h + w], z, ACT.Relu, bias=bo1[:, 0:1])
                    nc.scalar.activation(a, z, ACT.Abs, bias=bo1[:, 0:1]).then_inc(s_so, 1)
                    act.wait_ge(s_so, k + 1)
                    nc.scalar.activation(a, a, ACT.Exp, scale=-1.0).then_inc(s_eo, 1)
                    act.wait_ge(s_eo, k + 1)
                    nc.scalar.activation(a, a, ACT.Ln, bias=1.0).then_inc(s_lo1, 1)
        @block.vector
        def _(dve):
            chain = [0]

            def link(ins):
                chain[0] += 1
                ins.then_inc(s_chain, 1)
                dve.wait_ge(s_chain, chain[0])

            V = nc.vector
            V.memset(ones[:, :], 1.0)
            V.memset(attrT[64:96, :, :], 1.0).then_inc(s_ones, 1)
            V.memset(ones_bf[:, :], 1.0)
            dve.wait_ge(s_iota, 2)
            V.tensor_scalar(ident[:, :], column_no[:, :], row_no[:, 0:1], None, ALU.is_equal)
            V.tensor_scalar(earlier[:, :], column_no[:, :], row_no[:, 0:1], None, ALU.is_lt)
            for k in range(3):
                V.tensor_scalar(is_row[:, k:k + 1], row_no[:, 0:1], float(k), None, ALU.is_equal)
            V.tensor_scalar(spare_row[:, :], row_no[:, 0:1], float(N), None, ALU.add).then_inc(s_const, 1)
            dve.wait_ge(s_const, 1)

            dve.wait_ge(s_xs, 16 * (1 if NLAST == P else 2))
            V.memset(meanvar[:, :, :], 0.0).then_inc(s_chain, 1)
            for b in range(NB):
                r = P if b < NB - 1 else NLAST
                last = V.bn_stats(stats[0:r, b, :], xs[0:r, b, :])
            chain[0] += 2
            last.then_inc(s_chain, 1)
            dve.wait_ge(s_chain, chain[0])
            for b in range(NB):
                r = P if b < NB - 1 else NLAST
                last = V.bn_aggr(meanvar[0:r, b, :], stats[0:r, b, :])
            link(last)
            V.tensor_scalar(std[:, :], meanvar[:, :, 1], 1e-5, None, ALU.add).then_inc(s_var, 1)

            for k in (1, 0):
                dve.wait_ge(s_chunks[k], 16 * ndma)
                for g in range(G):
                    last = V.tensor_copy(chunk_16[0:rows_of[g], k, g, :].rearrange("c (t p) -> c p t", t=T),
                                         chunk_i[0:rows_of[g], k, g, :].rearrange("c (p t) -> c p t", t=T))
                last.then_inc(s_ch16, 1)
                if k == 1:
                    dve.wait_ge(s_std, 1)
                    link(V.reciprocal(rstd[:, :], std[:, :]))
                    for b in range(NB):
                        r = P if b < NB - 1 else NLAST
                        last = V.tensor_scalar(normed[0:r, b, :], xs[0:r, b, :], meanvar[0:r, b, 0:1], rstd[0:r, b:b + 1],
                                               ALU.subtract, ALU.mult)
                        if b % 4 == 3 or b == NB - 1:
                            last.then_inc(s_norm, 1)

            def rest_of(q):
                blocks, last = quad(q)
                n = len(blocks)
                r = P if n > 1 else last
                dve.wait_ge(s_hi, q + 1)
                if q >= 2:
                    dve.wait_ge(s_mid, q - 1)
                V.tensor_tensor(rest[0:r, q % 2, 0:n * F].rearrange("p (b f) -> p b f", f=F),
                                ps[2 + q % 2][0:r, 0:n * F].rearrange("p (b f) -> p b f", f=F),
                                parts[0:r, q % 2, 0:n, 0, :], ALU.subtract).then_inc(s_rest, 1)

            def low(q):
                blocks, last = quad(q)
                n = len(blocks)
                r = P if n > 1 else last
                dve.wait_ge(s_mid, q + 1)
                V.tensor_tensor(parts[0:r, q % 2, 0:n, 2, :],
                                rest[0:r, q % 2, 0:n * F].rearrange("p (b f) -> p b f", f=F),
                                parts[0:r, q % 2, 0:n, 1, :], ALU.subtract).then_inc(s_lo, 1)

            for q in range(NQ + 1):
                if q < NQ:
                    rest_of(q)
                if q >= 1:
                    low(q - 1)

            for k in (1, 0):
                for g in range(G):
                    last = V.tensor_copy(chunk_f[0:rows_of[g], k, g, :], chunk_i[0:rows_of[g], k, g, :])
                last.then_inc(s_chf, 1)
            dve.wait_ge(s_chf, 1)
            for g in range(G):
                r = rows_of[g]
                V.tensor_reduce(dst_min[0:r, g:g + 1], chunk_f[0:r, 1, g, :], AX.X, ALU.min)
                last = V.tensor_reduce(dst_max[0:r, g:g + 1], chunk_f[0:r, 1, g, :], AX.X, ALU.max)
            link(last)
            for g in range(G):
                last = V.tensor_scalar(dst_min[0:rows_of[g], g:g + 1], dst_min[0:rows_of[g], g:g + 1], float(N - P), None, ALU.min)
            link(last)
            for g in range(G):
                r = rows_of[g]
                last = V.tensor_tensor(spread[0:r, g:g + 1], dst_max[0:r, g:g + 1], dst_min[0:r, g:g + 1], ALU.subtract)
            link(last)
            for g in range(G):
                r = rows_of[g]
                V.tensor_scalar(diag[0:r, g, 0, 0:r], ident[0:r, 0:r], dst_min[0:r, g:g + 1], None, ALU.mult)
                last = V.tensor_scalar(diag[0:r, g, 1, 0:r], ident[0:r, 0:r], spread[0:r, g:g + 1], None, ALU.mult)
            last.then_inc(s_diag, 1)

            for n, k in enumerate((1, 0, 2)):
                col = (src_col, dst_col, cut_col)[k]
                for g in range(G):
                    j, r = n * G + g, rows_of[g]
                    dve.wait_ge(s_colps, j + 1)
                    V.tensor_copy(col[:, g * P:g * P + r, :],
                                  ps[4 + j % 2][:, 0:T * r].rearrange("p (t c) -> p c t", t=T)).then_inc(s_col, 1)
            dve.wait_ge(s_col, 3 * G)
            if REPEATED:
                V.memset(cut_col[0:REPEATED // T, NCH - 1, :], 0.0)
            V.tensor_scalar(src_less_spare[:, 0:NCH, :], src_col[:, 0:NCH, :], spare_row[:, 0:1], None, ALU.subtract)

            dve.wait_ge(s_bps, 1)
            V.tensor_scalar(window_col[:, 0:NCH], ps[6][:, 0:NCH], row_no[:, 0:1], None, ALU.add)
            V.tensor_copy(base_row[0:1, 0:NCH], ps[6][0:1, 0:NCH]).then_inc(s_base, 1)
            link(V.tensor_reduce(far[0:1, 0:1], ps[7][0:1, 0:NCH], AX.X, ALU.max))
            V.tensor_scalar(in_order[0:1, 0:1], far[0:1, 0:1], float(P), None, ALU.is_lt).then_inc(s_flag, 1)

            dve.wait_ge(s_w, 16 * (7 + 2 * T))
            dve.wait_ge(s_bias, 1)
            V.scalar_tensor_tensor(bo2_row[:, :], ps[4][:, F:2 * F], -LN2, bo2_row[:, :], ALU.mult, ALU.add)
            link(V.scalar_tensor_tensor(bf2_row[:, :], ps[4][:, 0:F], -LN2, bf2_row[:, :], ALU.mult, ALU.add))
            link(V.tensor_copy(bf2_hi[:, :], bf2_row[:, :]))
            link(V.tensor_tensor(bf2_rest[:, :], bf2_row[:, :], bf2_hi[:, :], ALU.subtract))
            link(V.tensor_copy(bf2_mid[:, :], bf2_rest[:, :]))
            V.tensor_scalar(bf2_sum[:, :], bf2_hi[:, :], is_row[:, 0:1], None, ALU.mult)
            link(V.tensor_tensor(bf2_rest[:, :], bf2_rest[:, :], bf2_mid[:, :], ALU.subtract))
            link(V.scalar_tensor_tensor(bf2_sum[:, :], bf2_mid[:, :], is_row[:, 1:2], bf2_sum[:, :], ALU.mult, ALU.add))
            for t in range(T):
                last = V.scalar_tensor_tensor(bf2_parts[:, t, :], bf2_rest[:, :], is_row[:, 2:3], bf2_sum[:, :], ALU.mult, ALU.add)
            last.then_inc(s_biasr, 1)
            dve.wait_ge(s_biasr, 1)

            def work(in_order):
                def step(i, m):
                    c, slot, odd = i + 1, (m + 1) % 4, (m + 1) % 2
                    if in_order and exists(c):
                        after_slot(dve, s_dstb, c, slot)
                        after(dve, s_xgp, c - 2)
                        V.tensor_scalar(onehot[:, odd, :], dst_b[:, slot, :], window_col[:, bass.ds(c, 1)], None,
                                        ALU.is_equal).then_inc(s_oh, 1)
                    if not in_order and exists(c):
                        after_slot(dve, s_gath, c - 4, slot, T)
                        V.tensor_copy(dst_now[:, slot, :], dst_col[:, bass.ds(c, 1), :].rearrange("p o t -> p (o t)")).then_inc(s_dnow, 1)
                    if exists(i + 1):
                        after(dve, s_log, i + 1)
                        after(dve, s_fp, i - 1)
                        V.scalar_tensor_tensor(hidden[:, (m + 1) % 2, :], hidden_ps[:, :], 0.0, hidden_exp[:, (m + 1) % 2, :],
                                               ALU.max, ALU.add).then_inc(s_h, 1)
                    c, slot, odd = i, m, m % 2
                    if exists(c):
                        after_slot(dve, s_srcb, c, slot)
                        after(dve, s_sp, c - 2)
                        for t in range(T):
                            last = V.tensor_scalar(same[:, odd, t * P:(t + 1) * P], src_b[:, slot, t * P:(t + 1) * P],
                                                   src_col[:, bass.ds(c, 1), t], cut_col[:, bass.ds(c, 1), t],
                                                   ALU.is_equal, ALU.mult)
                        last.then_inc(s_same, 1)
                        for t in range(T):
                            last = V.scalar_tensor_tensor(same_earlier[:, odd, t * P:(t + 1) * P], src_b[:, slot, t * P:(t + 1) * P],
                                                          src_col[:, bass.ds(c, 1), t], earlier[:, :],
                                                          ALU.is_equal, ALU.mult, accum_out=n_earlier[:, slot, t:t + 1])
                        last.then_inc(s_first, 1)
                        if not in_order:
                            after_slot(dve, s_gath, c, slot, T)
                            after(dve, s_msg, c - 2)
                            g = gathered[:, slot, :, :]
                            V.tensor_tensor(xg[:, odd, :].rearrange("p (t f) -> p t f", t=T), g[:, :, 0:F], g[:, :, F:2 * F],
                                            ALU.add).then_inc(s_xgp, 1)
                            after(dve, s_xgp, c)
                            V.tensor_tensor(xg[:, odd, :].rearrange("p (t f) -> p t f", t=T),
                                            xg[:, odd, :].rearrange("p (t f) -> p t f", t=T), g[:, :, 2 * F:3 * F],
                                            ALU.add).then_inc(s_xg, 1)
                        after(dve, s_fp, c)
                        after(dve, s_xg, c)
                        V.tensor_tensor(message[:, odd, :], filter_ps[odd][:, :], xg[:, odd, :], ALU.mult).then_inc(s_msg, 1)
                        after(dve, s_first, c)
                        V.scalar_tensor_tensor(picked[:, slot, :], n_earlier[:, slot, :], 0.0,
                                               src_less_spare[:, bass.ds(c, 1), :].rearrange("p o t -> p (o t)"),
                                               ALU.is_equal, ALU.mult).then_inc(s_pick, 1)
                        after(dve, s_pick, c)
                        for t in range(T):
                            after(dve, s_scat[t], c - 4, 16)
                        V.tensor_scalar(target[:, slot, :], picked[:, slot, :], spare_row[:, 0:1], None,
                                        ALU.add).then_inc(s_idx, 1)
                steps(dve, step)
            both_orders(dve, lambda: dve.value_load(in_order[0:1, 0:1], min_val=0, max_val=1), work)

            V.tensor_tensor(xs[:, 0:NB - 1, :], xs[:, 0:NB - 1, :],
                            bo2_row[:, :].unsqueeze(1).to_broadcast([P, NB - 1, F]), ALU.add)
            V.tensor_tensor(xs[0:NLAST, NB - 1, :], xs[0:NLAST, NB - 1, :], bo2_row[0:NLAST, :], ALU.add).then_inc(s_res, 1)
            dve.wait_ge(s_res, 1)

            def add_up(q):
                n, h = len(piece(q)), q % 2
                dve.wait_ge(s_ald[h], 16 * T * (q // 2 + 1))
                if q >= 2:
                    dve.wait_ge(s_tp, q - 1)
                link(V.tensor_tensor(total[:, h, 0:n, :], acc_sb[:, h, 0, 0:n, :], acc_sb[:, h, 1, 0:n, :], ALU.add))
                link(V.tensor_tensor(total[:, h, 0:n, :], total[:, h, 0:n, :], acc_sb[:, h, 2, 0:n, :], ALU.add))
                V.tensor_tensor(total[:, h, 0:n, :], total[:, h, 0:n, :], acc_sb[:, h, 3, 0:n, :], ALU.add).then_inc(s_add, 1)

            def transposed(q):
                n, h = len(piece(q)) * P, q % 2
                dve.wait_ge(s_tp, q + 1)
                if q >= 2:
                    dve.wait_ge(s_o1, (q - 1) * (EB * P // 512))
                for k in range(0, n, 512):
                    w = min(512, n - k)
                    last = V.tensor_copy(totalT[:, h, k:k + w], ps[2 + k // 512][:, 0:w])
                last.then_inc(s_t, 1)

            def out_hidden(q):
                n, h = len(piece(q)) * P, q % 2
                for k in range(0, n, 512):
                    w, j = min(512, n - k), q * (EB * P // 512) + k // 512
                    dve.wait_ge(s_lo1, j + 1)
                    if q >= 2:
                        dve.wait_ge(s_o2, j - 3)
                    V.tensor_tensor(hid_o[:, h, k:k + w], relu_o[:, h, k:k + w], size_o[:, h, k:k + w], ALU.add).then_inc(s_o1s, 1)

            def finish(q):
                b, h = piece(q), q % 2
                dve.wait_ge(s_o2, min((q + 1) * (EB * P // 512), o2_count))
                if q >= 2:
                    dve.wait_ge(s_ost[h], 16 * stores_until(q - 1, h))
                for k in range(0, len(b), 4):
                    w = min(4, len(b) - k)
                    full = w if (b[k + w - 1] < NB - 1 or NLAST == P) else w - 1
                    if full:
                        last = V.tensor_tensor(out_sb[:, h, k:k + full, :],
                                               ps[6 + k // 4][:, 0:full * F].rearrange("p (b f) -> p b f", f=F),
                                               xs[:, b[k]:b[k] + full, :], ALU.add)
                    if full < w:
                        last = V.tensor_tensor(out_sb[0:NLAST, h, k + full, :], ps[6 + k // 4][0:NLAST, full * F:w * F],
                                               xs[0:NLAST, NB - 1, :], ALU.add)
                last.then_inc(s_o, 1)

            for q in range(NPC + 1):
                if q < NPC:
                    add_up(q)
                    transposed(q)
                if q >= 1:
                    out_hidden(q - 1)
                    finish(q - 1)


        @block.tensor
        def _(pe):
            MM, TR = nc.tensor.matmul, nc.tensor.transpose
            pe.wait_ge(s_const, 1)

            def tr(q):
                blocks, last = quad(q)
                pe.wait_ge(s_norm, q + 1)
                if q >= 2:
                    pe.wait_ge(s_hT, q - 1)
                for j, b in enumerate(blocks):
                    r = last if j == len(blocks) - 1 else P
                    ins = TR(ps[q % 2][:, j * P:j * P + r], normed[0:r, b, :], ident[0:r, 0:r])
                ins.then_inc(s_tr, 1)

            def product(q):
                blocks, last = quad(q)
                pe.wait_ge(s_hT, q + 1)
                if q >= 2:
                    pe.wait_ge(s_rest, q - 1)
                for j, b in enumerate(blocks):
                    r = last if j == len(blocks) - 1 else P
                    ins = MM(ps[2 + q % 2][0:r, j * F:(j + 1) * F], hT[:, q % 2, j * P:j * P + r], w_in[:, :], start=True, stop=True)
                ins.then_inc(s_xw, 1)

            pe.wait_ge(s_w, 16 * (7 + 2 * T))
            for q in range(NQ + 1):
                if q < NQ:
                    tr(q)
                if q >= 1:
                    product(q - 1)

            for n, k in enumerate((1, 0, 2)):
                if k < 2:
                    pe.wait_ge(s_chf, 2 - k)
                else:
                    pe.wait_ge(s_chunks[2], 16 * ndma)
                for g in range(G):
                    j, r = n * G + g, rows_of[g]
                    if j >= 2:
                        pe.wait_ge(s_col, j - 1)
                    for t in range(T):
                        ins = TR(ps[4 + j % 2][:, t * r:(t + 1) * r],
                                 chunk_f[0:r, k, g, :].rearrange("c (p t) -> c t p", t=T)[:, t, :], ident[0:r, 0:r])
                    ins.then_inc(s_colps, 1)
            pe.wait_ge(s_diag, 1)
            for k in range(2):
                for g in range(G):
                    r = rows_of[g]
                    ins = MM(ps[6 + k][:, g * P:g * P + r], ones[0:r, :], diag[0:r, g, k, 0:r], start=True, stop=True)
            ins.then_inc(s_bps, 1)
            pe.wait_ge(s_col, 3 * G)
            MM(ps[4][:, 0:F], ones[:, :], w_f2[:, :], start=True, stop=True)
            MM(ps[4][:, F:2 * F], ones[:, :], w_o2[:, :], start=True, stop=True).then_inc(s_bias, 1)
            pe.wait_ge(s_biasr, 1)

            def products(in_order):
                def step(i, m):
                    c, slot, odd = i + 2, (m + 2) % 4, m % 2
                    if exists(c):
                        after_slot(pe, s_attr, c, slot)
                        after(pe, s_aT, c - 1)
                        TR(attrT_ps[0:KA, odd * P:odd * P + P], attr[:, slot, :], ident[:, :]).then_inc(s_aTp, 1)
                    c, odd = i + 1, (m + 1) % 2
                    if exists(c):
                        after(pe, s_aT, c)
                        after(pe, s_h, c - 1)
                        for t in range(T):
                            ins = MM(hidden_ps[:, t * P:(t + 1) * P], w_f1[:, t, :], attrT[0:KA + 1, odd, :], start=True, stop=True)
                        ins.then_inc(s_hp, 1)
                    c, slot, odd = i, m, m % 2
                    if in_order and exists(c):
                        after(pe, s_oh, c)
                        after_slot(pe, s_xwin, c, slot)
                        after(pe, s_xg, c - 2)
                        for t in range(T):
                            for k in range(3):
                                ins = MM(xg_ps[odd][:, t * F:(t + 1) * F], onehot[:, odd, t * P:(t + 1) * P],
                                         xwin[:, slot, k * F:(k + 1) * F], start=(k == 0), stop=(k == 2))
                        ins.then_inc(s_xgp, 1)
                    if exists(c):
                        after(pe, s_h, c)
                        after(pe, s_msg, c - 2)
                        MM(filter_ps[odd][:, :], ones_bf[:, :], bf2_parts[:, :, :].rearrange("p t f -> p (t f)"),
                           start=True, stop=False, skip_group_check=True)
                        for t in range(T):
                            ins = MM(filter_ps[odd][:, t * F:(t + 1) * F], hidden[:, odd, t * P:(t + 1) * P], w_f2[:, :],
                                     start=False, stop=(t == T - 1), skip_group_check=True)
                        ins.then_inc(s_fp, 1)
                    c, odd = i - 1, (m - 1) % 2
                    if exists(c):
                        after(pe, s_same, c)
                        after(pe, s_msg, c)
                        after(pe, s_s, c - 2)
                        for t in range(T):
                            ins = MM(summed_ps[odd][:, t * F:(t + 1) * F], same[:, odd, t * P:(t + 1) * P],
                                     message[:, odd, t * F:(t + 1) * F], start=True, stop=True)
                        ins.then_inc(s_sp, 1)
                steps(pe, step)
            both_orders(pe, lambda: pe.value_load(in_order[0:1, 0:1], min_val=0, max_val=1), products)

            def total_tr(q):
                n, h = len(piece(q)), q % 2
                pe.wait_ge(s_add, q + 1)
                if q >= 1:
                    pe.wait_ge(s_t, q)
                for j in range(n):
                    ins = TR(ps[2 + j // 4][:, j % 4 * P:(j % 4 + 1) * P], total[:, h, j, :], ident[:, :])
                ins.then_inc(s_tp, 1)

            def out_products(q):
                n, h = len(piece(q)) * P, q % 2
                pe.wait_ge(s_t, q + 1)
                for k in range(0, n, 512):
                    w, j = min(512, n - k), q * (EB * P // 512) + k // 512
                    if q >= 1:
                        pe.wait_ge(s_o1s, j - 1)
                    MM(ps[4 + k // 512][:, 0:w], w_o1[:, :], totalT[:, h, k:k + w], start=True, stop=True).then_inc(s_o1, 1)
                if q >= 1:
                    pe.wait_ge(s_o, q)
                for k in range(0, n, 512):
                    w, j = min(512, n - k), q * (EB * P // 512) + k // 512
                    pe.wait_ge(s_o1s, j + 1)
                    for b in range(w // P):
                        ins = MM(ps[6 + k // 512][:, b * F:(b + 1) * F], hid_o[:, h, k + b * P:k + (b + 1) * P], w_o2[:, :],
                                 start=True, stop=True)
                    ins.then_inc(s_o2, 1)

            for q in range(NPC + 1):
                if q < NPC:
                    total_tr(q)
                if q >= 1:
                    out_products(q - 1)


_INS = ['x', 'src', 'dst', 'edge_attr_20', 'edge_weight1', 'L0_gnn_W_in', 'L0_gnn_W_f1', 'L0_gnn_b_f1', 'L0_gnn_W_f2',
        'L0_gnn_b_f2', 'L0_gnn_W_o1', 'L0_gnn_b_o1', 'L0_gnn_W_o2', 'L0_gnn_b_o2']


def kernel(**inputs):
    import numpy as _np
    import concourse.bacc as _bacc
    from concourse import mybir as _mybir
    from concourse.bass_utils import run_bass_kernel_spmd as _run

    nc = _bacc.Bacc("TRN2", target_bir_lowering=False, num_devices=1)
    arrays, args = {}, []
    for name in _INS:
        a = _np.ascontiguousarray(inputs[name])
        arrays[f"in_{name}_dram"] = a
        args.append(nc.dram_tensor(f"in_{name}_dram", a.shape, _mybir.dt.from_np(a.dtype), kind="ExternalInput").ap())
    shape = arrays["in_x_dram"].shape
    args.append(nc.dram_tensor("out_dram", shape, _mybir.dt.float32, kind="ExternalOutput").ap())
    gnn_kernel(nc, *args)
    r = _run(nc, [arrays], core_ids=[0])
    return r.results[0]["out_dram"]
```

```python
from contextlib import ExitStack
import math

import concourse.bass as bass
from concourse import mybir

P = 128
T = 4
CE = P * T
LAST_PEELED = 6
UNROLL = 4


def gnn_kernel(nc, x, src, dst, edge_attr, cutoff, W_in, W_f1, b_f1, W_f2, b_f2, W_o1, b_o1, W_o2, b_o2, out):
    fp32, bf16, i32, i16 = mybir.dt.float32, mybir.dt.bfloat16, mybir.dt.int32, mybir.dt.int16
    ALU, ACT, AX = mybir.AluOpType, mybir.ActivationFunctionType, mybir.AxisListType

    N, F = x.shape
    E, RBF = edge_attr.shape
    NCH = -(-E // CE)
    TAIL = E - CE
    REPEATED = (NCH - 1) * CE - TAIL
    assert REPEATED % T == 0 and REPEATED // T in (0, 32, 48, 64, 96) and F == P
    G = -(-NCH // P)
    rows_of = [min(P, NCH - g * P) for g in range(G)]
    NB = -(-N // P)
    NLAST = N - (NB - 1) * P
    NQ = -(-NB // 4)
    EB = 3
    NPC = -(-NB // EB)
    assert NLAST == P or (NB % 4 == 1 and NB % EB == 1)
    ACC_ROWS = -(-(N + P) // (10 * P)) * 10 * P
    LN2 = math.log(2.0)

    acc = [nc.dram_tensor(f"acc{t}", (ACC_ROWS, F), fp32, kind="Internal").ap() for t in range(T)]
    xw_parts = nc.dram_tensor("xw_parts", (N, 3 * F), bf16, kind="Internal").ap()
    src_rows = nc.dram_tensor("src_rows", (NCH, CE), i16, kind="Internal").ap()
    dst_rows = nc.dram_tensor("dst_rows", (NCH, CE), i16, kind="Internal").ap()

    ctx = ExitStack()
    with ctx:
        def sb(name, shape, dt=fp32):
            return ctx.enter_context(nc.sbuf_tensor(name, shape, dt))

        def pb(name, shape, dt=fp32):
            return ctx.enter_context(nc.psum_tensor(name, shape, dt))

        def sem(name):
            return ctx.enter_context(nc.semaphore(name))

        ident = sb("ident", [P, P])
        ones = sb("ones", [P, P])
        ones_bf = sb("ones_bf", [P, P], bf16)
        column_no = sb("column_no", [P, P])
        row_no = sb("row_no", [P, 1])
        is_row = sb("is_row", [P, 3])
        earlier = sb("earlier", [P, P])
        spare_row = sb("spare_row", [P, 1])
        w_in = sb("w_in", [P, F])
        KA = T * RBF
        w_f1 = sb("w_f1", [KA + 1, T, F])
        w_f2 = sb("w_f2", [P, F])
        w_o1 = sb("w_o1", [P, F])
        w_o2 = sb("w_o2", [P, F])
        bo1 = sb("bo1", [P, 1])
        bo1_negative = sb("bo1_negative", [P, 1])
        bo1_less_ln2 = sb("bo1_less_ln2", [P, P])
        bf2_row = sb("bf2_row", [P, F])
        bo2_row = sb("bo2_row", [P, F])
        bf2_hi = sb("bf2_hi", [P, F], bf16)
        bf2_mid = sb("bf2_mid", [P, F], bf16)
        bf2_rest = sb("bf2_rest", [P, F])
        bf2_sum = sb("bf2_sum", [P, F])
        bf2_parts = sb("bf2_parts", [P, T, F], bf16)
        ZB = 10
        assert ACC_ROWS // P % ZB == 0
        NZ = ACC_ROWS // P // ZB
        zeros = sb("zeros", [P, ZB * F])
        xs = sb("xs", [P, NB, F])
        stats = sb("stats", [P, NB, 6])
        meanvar = sb("meanvar", [P, NB, 2])
        std = sb("std", [P, NB])
        rstd = sb("rstd", [P, NB])
        shared_a = sb("shared_a", [P, max(NB * F + 3 * 4 * F, 4 * T * EB * F, 14 * CE)])
        shared_b = sb("shared_b", [P, max(3 * G * CE, 3 * 2 * EB * F)])
        shared_c = sb("shared_c", [P, max(2 * G * CE, 2 * EB * F)])
        normed = shared_a[:, 0:NB * F].rearrange("p (b f) -> p b f", f=F)
        hT = sb("hT", [P, 2, 4 * P])
        rest = shared_a[:, NB * F:NB * F + 3 * 4 * F].rearrange("p (h n) -> p h n", h=3)
        shared_d = sb("shared_d", [P, 4 * T * 3 * F], bf16)
        parts = shared_d[:, :].rearrange("p (h b k f) -> p h b k f", h=4, b=4, k=3)
        gathered = shared_d[:, :].rearrange("p (s t c) -> p s t c", s=4, t=T)
        chunk_i = shared_c[:, 0:2 * G * CE].bitcast(i32).rearrange("p (k g e) -> p k g e", k=2, g=G)
        chunk_f = shared_b[:, 0:3 * G * CE].rearrange("p (k g e) -> p k g e", k=3, g=G)
        shared_e = sb("shared_e", [P, max(G * CE, 2 * EB * F)])
        chunk_16 = shared_e[:, 0:G * CE].bitcast(i16).rearrange("p (k g e) -> p k g e", k=2, g=G)
        dst_min = sb("dst_min", [P, G])
        dst_max = sb("dst_max", [P, G])
        spread = sb("spread", [P, G])
        diag = sb("diag", [P, G, 2, P])
        src_col = sb("src_col", [P, G * P, T])
        src_less_spare = sb("src_less_spare", [P, G * P, T])
        cut_col = sb("cut_col", [P, G * P, T])
        dst_col = sb("dst_col", [P, G * P, T], i32)
        window_col = sb("window_col", [P, G * P])
        base_row = sb("base_row", [1, G * P], i32)
        widest = sb("widest", [1, 1])
        in_order = sb("in_order", [1, 1], i32)
        attr = sb("attr", [P, 4, T * RBF])
        dst_b = sb("dst_b", [P, 4, CE], i16)
        src_b = sb("src_b", [P, 4, CE], i16)
        xwin = sb("xwin", [P, 4, 3 * F], bf16)
        dst_now = sb("dst_now", [P, 4, T], i32)
        attrT = sb("attrT", [96, 2, P])
        onehot = sb("onehot", [P, 2, CE], bf16)
        two_parts = onehot[:, :, :].rearrange("p h e -> p (h e)").bitcast(fp32).rearrange("p (t f) -> p t f", t=T)
        same_earlier = sb("same_earlier", [P, 2, CE], bf16)
        n_earlier = sb("n_earlier", [P, 4, T])
        picked = sb("picked", [P, 4, T])
        target = sb("target", [P, 4, T], i32)
        hidden_exp, hidden, xg, message, same = (
            shared_a[:, k * 2 * CE:(k + 1) * 2 * CE].rearrange("p (h e) -> p h e", h=2) for k in range(5))
        summed = shared_a[:, 10 * CE:14 * CE].rearrange("p (s e) -> p s e", s=4)
        acc_sb = shared_a[:, 0:4 * T * EB * F].rearrange("p (h t n) -> p h t n", h=4, t=T)
        total, totalT, log_o = (shared_b[:, k * 2 * EB * F:(k + 1) * 2 * EB * F].rearrange("p (h n) -> p h n", h=2) for k in range(3))
        hid_o = shared_c[:, 0:2 * EB * F].rearrange("p (h n) -> p h n", h=2)
        out_sb = shared_e[:, 0:2 * EB * F].rearrange("p (h b f) -> p h b f", h=2, b=EB)

        ps = [pb(f"ps{i}", [P, 512]) for i in range(8)]
        attrT_ps, hidden_ps = ps[0], ps[1]
        filter_ps, xg_ps, summed_ps = ps[2:4], ps[4:6], ps[6:8]

        s_xs = [sem(f"x_loaded{k}") for k in range(4)]
        s_w = sem("weights_loaded")
        s_chunks = [sem("src_loaded"), sem("dst_loaded"), sem("cutoff_loaded")]
        s_iota = sem("iota_done")
        s_const = sem("constants_ready")
        s_w1z = sem("w_f1_cleared")
        s_zero = sem("zeros_ready")
        s_accz = sem("accumulators_cleared")
        s_less = sem("src_less_spare_ready")
        s_var = sem("variance_ready")
        s_std = sem("std_ready")
        s_chain = sem("dve_chain")
        s_norm = sem("normed_ready")
        s_tr = sem("hT_in_psum")
        s_hT = sem("hT_ready")
        s_xw = sem("xw_in_psum")
        s_hi = sem("xw_hi_ready")
        s_rest = sem("xw_rest_ready")
        s_mid = sem("xw_mid_ready")
        s_lo = sem("xw_lo_ready")
        s_lo_pool = sem("xw_lo_ready_of_gpsimd")
        s_parts = [sem(f"xw_parts_stored{k}") for k in range(4)]
        s_shift = sem("bo1_less_ln2_ready")
        s_bias = sem("bias_sums_in_psum")
        s_biasr = sem("bias_rows_ready")
        s_ch16 = sem("chunk_rows_16_ready")
        s_rows = sem("chunk_rows_stored")
        s_chf = sem("chunk_rows_float_ready")
        s_colps = sem("columns_in_psum")
        s_col = sem("columns_ready")
        s_cut = sem("repeated_edges_cut")
        s_diag = sem("diagonals_ready")
        s_bps = sem("bases_in_psum")
        s_base = sem("bases_ready")
        s_flag = sem("order_flag_ready")
        s_attr = [sem(f"attr_loaded{k}") for k in range(4)]
        s_dstb = [sem(f"dst_loaded{k}") for k in range(4)]
        s_srcb = [sem(f"src_loaded{k}") for k in range(4)]
        s_xwin = [sem(f"window_loaded{k}") for k in range(4)]
        s_gath = [sem(f"rows_gathered{k}") for k in range(4)]
        s_scat = [sem(f"scattered{t}") for t in range(T)]
        s_aTp = sem("attrT_in_psum")
        s_aT = sem("attrT_ready")
        s_hp = sem("hidden_in_psum")
        s_size = sem("hidden_size_ready")
        s_exp = sem("hidden_exp_ready")
        s_log = sem("hidden_log_ready")
        s_h = sem("hidden_ready")
        s_ones = sem("attrT_ones_ready")
        s_oh = sem("onehot_ready")
        s_two = sem("two_parts_added")
        s_dnow = sem("dst_now_ready")
        s_same = sem("same_ready")
        s_first = sem("n_earlier_ready")
        s_go = sem("pool_may_go")
        s_sp_go = sem("sync_may_go")
        s_pick = sem("picked_ready")
        s_idx = sem("targets_ready")
        s_xgp = sem("xg_in_psum")
        s_xg = sem("xg_ready")
        s_fp = sem("filter_in_psum")
        s_msg = sem("message_ready")
        s_sp = sem("sums_in_psum")
        s_s = sem("sums_ready")
        s_ald = [sem(f"acc_loaded{k}") for k in range(4)]
        s_add01 = sem("acc_0_1_added")
        s_add23 = sem("acc_2_3_added")
        s_add = sem("acc_added")
        s_tp = sem("totalT_in_psum")
        s_t = sem("totalT_ready")
        s_o1 = sem("out_hidden_in_psum")
        s_so = sem("out_size_ready")
        s_eo = sem("out_exp_ready")
        s_lo1 = sem("out_log_ready")
        s_o1s = sem("out_hidden_ready")
        s_o2 = sem("out_in_psum")
        s_o = sem("out_ready")
        s_ost = [sem("out_stored_even"), sem("out_stored_odd")]
        s_res = sem("residual_ready")

        def quad(q):
            b = range(4 * q, min(4 * q + 4, NB))
            return b, (NLAST if b[-1] == NB - 1 and NLAST < P else P)

        def low_on_gpsimd(q):
            return q >= 4 and q % 2 == 0

        def low(q, eng, semaphore):
            blocks, last = quad(q)
            n = len(blocks)
            r = P if n > 1 else last
            eng.wait_ge(s_mid, q + 1)
            eng.tensor_tensor(parts[0:r, q % 4, 0:n, 2, :],
                              rest[0:r, q % 3, 0:n * F].rearrange("p (b f) -> p b f", f=F),
                              parts[0:r, q % 4, 0:n, 1, :], ALU.subtract).then_inc(semaphore, 1)

        def after_low(eng, q):
            n = sum(low_on_gpsimd(k) == low_on_gpsimd(q) for k in range(q + 1))
            eng.wait_ge(s_lo_pool if low_on_gpsimd(q) else s_lo, n)

        def piece(q):
            return range(EB * q, min(EB * q + EB, NB))

        def stores_until(q_end, h):
            return len(range(h, q_end, 2))

        x_pieces = [range(k * NB // 4, (k + 1) * NB // 4) for k in range(4)]
        parts_stored = [len(range(h, NQ, 4)) for h in range(4)]
        ndma = sum(1 for g in range(G) if min(rows_of[g], NCH - 1 - g * P) > 0) + 1

        def steps(eng, step):
            turns = max(0, (NCH - 2 - LAST_PEELED) // UNROLL)
            for i in range(-2, LAST_PEELED):
                step(i, i % 4)
            if turns:
                with eng.Fori(0, turns) as turn:
                    for j in range(UNROLL):
                        step(turn * UNROLL + (LAST_PEELED + j), (LAST_PEELED + j) % 4)
            for i in range(LAST_PEELED + turns * UNROLL, NCH + 1):
                step(i, i % 4)

        def known(c):
            return type(c) is int

        def exists(c):
            return not known(c) or 0 <= c < NCH

        def after(eng, semaphore, c, per=1):
            if not known(c) or c >= 0:
                eng.wait_ge(semaphore, c * per + per)

        def after_slot(eng, semaphores, c, slot, dmas=1):
            if not known(c) or c >= 0:
                eng.wait_ge(semaphores[slot], (c - slot) * (4 * dmas) + 16 * dmas)

        def both_orders(eng, value_of, body):
            eng.wait_ge(s_flag, 1)
            flag = value_of()
            with eng.If(flag == 1):
                body(True)
            with eng.Else():
                body(False)

        block = ctx.enter_context(nc.Block())

        @block.sync
        def _(sp):
            def load_nodes(k):
                b = x_pieces[k]
                whole = b if b[-1] < NB - 1 or NLAST == P else b[:-1]
                sp.dma_start(xs[:, whole[0]:whole[-1] + 1, :],
                             x[whole[0] * P:(whole[-1] + 1) * P, :].rearrange("(b p) f -> p b f", p=P)).then_inc(s_xs[k], 16)
                if len(whole) < len(b):
                    sp.dma_start(xs[0:NLAST, NB - 1, :], x[(NB - 1) * P:N, :]).then_inc(s_xs[k], 16)

            def load_chunks(k):
                a = (src, dst, cutoff.rearrange("e o -> (e o)"))[k]
                tile = chunk_f if k == 2 else chunk_i
                for g in range(G):
                    r = min(rows_of[g], NCH - 1 - g * P)
                    if r > 0:
                        sp.dma_start(tile[0:r, k, g, :], a[g * P * CE:(g * P + r) * CE].rearrange("(c e) -> c e", e=CE)).then_inc(s_chunks[k], 16)
                r = (NCH - 1) % P
                sp.dma_start(tile[r:r + 1, k, G - 1, :], a[TAIL:E].rearrange("(c e) -> c e", e=CE)).then_inc(s_chunks[k], 16)

            load_nodes(0)
            load_nodes(1)
            load_chunks(1)
            load_nodes(2)
            load_nodes(3)
            load_chunks(0)
            load_chunks(2)
            clears = [(t, k) for t in range(T) for k in range(NZ)]
            early = len(clears) // 2

            def clear(t, k):
                sp.dma_start(acc[t].rearrange("(k p r) f -> k p (r f)", p=P, r=ZB)[k], zeros[:, :]).then_inc(s_accz, 16)

            sp.wait_ge(s_zero, 1)
            for t, k in clears[0:early]:
                clear(t, k)
            def store_rows(n, k, a):
                for g in range(G):
                    sp.wait_ge(s_ch16, n * G + g + 1)
                    sp.dma_start(a[g * P:g * P + rows_of[g], :], chunk_16[0:rows_of[g], k, g, :]).then_inc(s_rows, 16)

            store_rows(0, 1, dst_rows)
            for j, (t, k) in enumerate(clears[early:]):
                sp.wait_ge(s_rest, min(j + 1, NQ))
                clear(t, k)
            store_rows(1, 0, src_rows)
            sp.wait_ge(s_rows, 16 * 2 * G)

            def loads(in_order):
                def step(i, m):
                    c, slot = i + 2, (m + 2) % 4
                    if exists(c):
                        after(sp, s_aTp, c - 4)
                        if known(c) and c == NCH - 1:
                            rows = edge_attr[TAIL:E, :]
                        else:
                            rows = edge_attr[bass.ds(c * CE, CE), :]
                        sp.dma_start(attr[:, slot, :], rows.rearrange("(p t) k -> p (t k)", t=T)).then_inc(s_attr[slot], 16)
                        after(sp, s_first, c - 4)
                        sp.sem_inc(s_sp_go, 1)
                        sp.dma_start(src_b[:, slot, :], src_rows[bass.ds(c, 1), :].to_broadcast([P, CE])).then_inc(s_srcb[slot], 16)
                        if in_order:
                            after(sp, s_oh, c - 4)
                            sp.dma_start(dst_b[:, slot, :], dst_rows[bass.ds(c, 1), :].to_broadcast([P, CE])).then_inc(s_dstb[slot], 16)
                    c, slot = i + 1, (m + 1) % 4
                    if in_order and exists(c):
                        base = sp.value_load(base_row[0:1, bass.ds(c, 1)], min_val=0, max_val=N - P)
                        after(sp, s_xgp, c - 4)
                        if known(c) and c == 0:
                            for h in range(4):
                                sp.wait_ge(s_parts[h], 16 * parts_stored[h])
                        sp.dma_start(xwin[:, slot, :], xw_parts[bass.ds(base, P), :]).then_inc(s_xwin[slot], 16)
                steps(sp, step)
            sp.wait_ge(s_base, 1)
            both_orders(sp, lambda: sp.value_load(in_order[0:1, 0:1], min_val=0, max_val=1), loads)

            for t in range(T):
                sp.wait_ge(s_scat[t], 16 * NCH)
            for q in range(NPC):
                b = piece(q)
                if q >= 4:
                    sp.wait_ge(s_add, q - 3)
                for t in range(T):
                    sp.dma_start(acc_sb[:, q % 4, t, 0:len(b) * F].rearrange("p (b f) -> p b f", f=F),
                                 acc[t][b[0] * P:(b[-1] + 1) * P, :].rearrange("(b p) f -> p b f", p=P)).then_inc(s_ald[q % 4], 16)

        @block.gpsimd
        def _(pool):
            nc.gpsimd.iota(column_no[:, :], [[1, P]], base=0, channel_multiplier=0,
                           allow_small_or_imprecise_dtypes=True).then_inc(s_iota, 1)
            nc.gpsimd.iota(row_no[:, :], [[0, 1]], base=0, channel_multiplier=1,
                           allow_small_or_imprecise_dtypes=True).then_inc(s_iota, 1)
            nc.gpsimd.memset(w_f1[:, :, :], 0.0).then_inc(s_w1z, 1)
            nc.gpsimd.memset(zeros[:, :], 0.0).then_inc(s_zero, 1)

            def to_float(k, g):
                return nc.gpsimd.tensor_copy(chunk_f[0:rows_of[g], k, g, :], chunk_i[0:rows_of[g], k, g, :])

            def to_16_bits(k, g):
                return nc.gpsimd.tensor_copy(chunk_16[0:rows_of[g], k, g, :].rearrange("c (t p) -> c p t", t=T),
                                             chunk_i[0:rows_of[g], k, g, :].rearrange("c (p t) -> c p t", t=T))

            pool.wait_ge(s_chunks[1], 16 * ndma)
            for g in range(G):
                to_float(1, g).then_inc(s_chf, 1)
            for g in range(G):
                to_16_bits(1, g).then_inc(s_ch16, 1)
            pool.wait_ge(s_chunks[0], 16 * ndma)
            for g in range(G):
                to_float(0, g).then_inc(s_chf, 1)

            for q in range(max(NQ, G)):
                if q < G:
                    to_16_bits(0, q).then_inc(s_ch16, 1)
                if q >= NQ:
                    continue
                blocks, last = quad(q)
                if low_on_gpsimd(q):
                    low(q, pool, s_lo_pool)
                after_low(pool, q)
                if last == P:
                    pool.dma_start(xw_parts[4 * q * P:(4 * q + len(blocks)) * P, :].rearrange("(b p) c -> p b c", p=P),
                                   parts[:, q % 4, 0:len(blocks), :, :].rearrange("p b k f -> p b (k f)")).then_inc(s_parts[q % 4], 16)
                else:
                    pool.dma_start(xw_parts[blocks[-1] * P:N, :],
                                   parts[0:last, q % 4, 0, :, :].rearrange("p k f -> p (k f)")).then_inc(s_parts[q % 4], 16)
            pool.wait_ge(s_col, 3 * G)
            pool.wait_ge(s_const, 1)
            nc.gpsimd.tensor_scalar(src_less_spare[:, 0:NCH, :], src_col[:, 0:NCH, :], spare_row[:, 0:1], None,
                                    ALU.subtract).then_inc(s_less, 1)
            for h in range(4):
                pool.wait_ge(s_parts[h], 16 * parts_stored[h])
            pool.wait_ge(s_accz, 16 * T * NZ)

            def scatters(in_order):
                def step(i, m):
                    c, slot = i + 1, (m + 1) % 4
                    if not in_order and exists(c):
                        after(pool, s_xgp, c - 4)
                        after(pool, s_dnow, c)
                        pool.sem_inc(s_go, 1)
                        for t in range(T):
                            nc.gpsimd.indirect_dma_start(
                                out=gathered[:, slot, t, :], out_offset=None, in_=xw_parts[:, :],
                                in_offset=bass.IndirectOffsetOnAxis(ap=dst_now[:, slot, t:t + 1], axis=0)).then_inc(s_gath[slot], 16)
                    c, slot = i - 1, (m - 1) % 4
                    if exists(c):
                        after(pool, s_idx, c)
                        after(pool, s_s, c)
                        for t in range(T):
                            after(pool, s_scat[t], c - 1, 16)
                            pool.sem_inc(s_go, 1)
                            nc.gpsimd.indirect_dma_start(
                                out=acc[t], out_offset=bass.IndirectOffsetOnAxis(ap=target[:, slot, t:t + 1], axis=0),
                                in_=summed[:, slot, t * F:(t + 1) * F], in_offset=None,
                                compute_op=ALU.add).then_inc(s_scat[t], 16)
                steps(pool, step)
            both_orders(pool, lambda: pool.value_load(in_order[0:1, 0:1], min_val=0, max_val=1), scatters)

            for q in range(NPC + 4):
                if q < NPC:
                    n, h = len(piece(q)) * F, q % 4
                    pool.wait_ge(s_ald[h], 16 * T * (q // 4 + 1))
                    nc.gpsimd.tensor_tensor(acc_sb[:, h, 2, 0:n], acc_sb[:, h, 2, 0:n], acc_sb[:, h, 3, 0:n], ALU.add).then_inc(s_add23, 1)
                if q >= 4:
                    b, h = piece(q - 4), q % 2
                    pool.wait_ge(s_o, q - 3)
                    if b[-1] == NB - 1 and NLAST < P:
                        pool.dma_start(out[b[-1] * P:N, :], out_sb[0:NLAST, h, 0, :]).then_inc(s_ost[h], 16)
                    else:
                        pool.dma_start(out[b[0] * P:(b[-1] + 1) * P, :].rearrange("(b p) f -> p b f", p=P),
                                       out_sb[:, h, 0:len(b), :]).then_inc(s_ost[h], 16)
            for h in range(2):
                pool.wait_ge(s_ost[h], 16 * stores_until(NPC, h))

        @block.scalar
        def _(act):
            for tile, a in ((w_in, W_in), (w_f2, W_f2), (w_o1, W_o1), (w_o2, W_o2)):
                act.dma_start(tile[:, :], a).then_inc(s_w, 16)
            act.dma_start(bo1[:, :], b_o1.rearrange("(p o) -> p o", o=1)).then_inc(s_w, 16)
            for tile, a in ((bf2_row, b_f2), (bo2_row, b_o2)):
                act.dma_start(tile[:, :], a.rearrange("(o f) -> o f", o=1).to_broadcast([P, F])).then_inc(s_w, 16)
            act.wait_ge(s_w1z, 1)
            for t in range(T):
                act.dma_start(w_f1[t * RBF:(t + 1) * RBF, t, :], W_f1).then_inc(s_w, 16)
                act.dma_start(w_f1[KA:KA + 1, t, :], b_f1.rearrange("(o f) -> o f", o=1)).then_inc(s_w, 16)

            def column(j):
                n, g = divmod(j, G)
                r = rows_of[g]
                act.wait_ge(s_colps, j + 1)
                nc.scalar.activation((dst_col, cut_col, src_col)[n][:, g * P:g * P + r, :],
                                     ps[4 + j % 2][:, 0:T * r].rearrange("p (t c) -> p c t", t=T), ACT.Copy).then_inc(s_col, 1)

            for j in range(G):
                column(j)
            act.wait_ge(s_var, 1)
            nc.scalar.activation(std[:, :], std[:, :], ACT.Sqrt).then_inc(s_std, 1)
            nc.scalar.preload_act_table_set("natural_log_exp_and_others")

            for j in range(G, 2 * G):
                column(j)

            def relu(q):
                blocks, last = quad(q)
                w = (len(blocks) - 1) * P + last
                act.wait_ge(s_tr, q + 1)
                if q >= 2:
                    act.wait_ge(s_xw, q - 1)
                nc.scalar.activation(hT[:, q % 2, 0:w], ps[q % 2][:, 0:w], ACT.Relu).then_inc(s_hT, 1)

            def high(q):
                blocks, last = quad(q)
                n = len(blocks)
                r = P if n > 1 else last
                act.wait_ge(s_xw, q + 1)
                if q >= 4:
                    act.wait_ge(s_parts[q % 4], 16 * (q // 4))
                nc.scalar.activation(parts[0:r, q % 4, 0:n, 0, :], ps[2 + q % 2][0:r, 0:n * F].rearrange("p (b f) -> p b f", f=F),
                                     ACT.Copy).then_inc(s_hi, 1)

            def middle(q):
                blocks, last = quad(q)
                n = len(blocks)
                r = P if n > 1 else last
                act.wait_ge(s_rest, q + 1)
                nc.scalar.activation(parts[0:r, q % 4, 0:n, 1, :], rest[0:r, q % 3, 0:n * F].rearrange("p (b f) -> p b f", f=F),
                                     ACT.Copy).then_inc(s_mid, 1)

            for q in range(NQ + 2):
                if q < NQ:
                    relu(q)
                if 1 <= q <= NQ:
                    high(q - 1)
                if 4 <= q < G + 4:
                    column(2 * G + q - 4)
                if q >= 2:
                    middle(q - 2)
            for q in range(max(NQ + 2, 4), G + 4):
                column(2 * G + q - 4)

            def evacuate(in_order):
                def step(i, m):
                    c = i + 2
                    if exists(c):
                        after(act, s_aTp, c)
                        after(act, s_hp, c - 2)
                        nc.scalar.activation(attrT[0:KA, m % 2, :], attrT_ps[0:KA, m % 2 * P:m % 2 * P + P],
                                             ACT.Copy).then_inc(s_aT, 1)
                    c, odd = i + 1, (m + 1) % 2
                    if exists(c):
                        after(act, s_hp, c)
                        after(act, s_h, c - 2)
                        nc.scalar.activation(hidden_exp[:, odd, :], hidden_ps[:, :], ACT.Abs).then_inc(s_size, 1)
                        after(act, s_size, c)
                        nc.scalar.activation(hidden_exp[:, odd, :], hidden_exp[:, odd, :], ACT.Exp, scale=-1.0).then_inc(s_exp, 1)
                        after(act, s_exp, c)
                        nc.scalar.activation(hidden_exp[:, odd, :], hidden_exp[:, odd, :], ACT.Ln, bias=1.0).then_inc(s_log, 1)
                    c, odd = i, m % 2
                    if exists(c):
                        after(act, s_xgp, c)
                        after(act, s_msg, c - 2)
                        for t in range(T):
                            last = nc.scalar.activation(xg[:, odd, t * F:(t + 1) * F], xg_ps[odd][:, t * F:(t + 1) * F], ACT.Copy,
                                                        scale=cut_col[:, bass.ds(c, 1), t])
                        last.then_inc(s_xg, 1)
                    c, odd, slot = i - 1, (m - 1) % 2, (m - 1) % 4
                    if exists(c):
                        after(act, s_sp, c)
                        for t in range(T):
                            after(act, s_scat[t], c - 4, 16)
                        nc.scalar.activation(summed[:, slot, :], summed_ps[odd][:, :], ACT.Copy).then_inc(s_s, 1)
                steps(act, step)
            act.wait_ge(s_ones, 1)
            if REPEATED:
                act.wait_ge(s_cut, 1)
            both_orders(act, lambda: act.value_load(in_order[0:1, 0:1], min_val=0, max_val=1), evacuate)

            for q in range(NPC + 1):
                if q < NPC:
                    n, h = len(piece(q)) * P, q % 2
                    act.wait_ge(s_tp, q + 1)
                    if q >= 2:
                        act.wait_ge(s_o1, q - 1)
                    nc.scalar.activation(totalT[:, h, 0:n], ps[2 + h][:, 0:n], ACT.Copy).then_inc(s_t, 1)
                if q >= 1:
                    k, h = q - 1, (q - 1) % 2
                    n = len(piece(k)) * P
                    act.wait_ge(s_o1, k + 1)
                    if k >= 2:
                        act.wait_ge(s_o1s, k - 1)
                    z, a = ps[4 + h][:, 0:n], log_o[:, h, 0:n]
                    nc.scalar.activation(a, z, ACT.Abs, bias=bo1[:, 0:1]).then_inc(s_so, 1)
                    act.wait_ge(s_so, k + 1)
                    nc.scalar.activation(a, a, ACT.Exp, scale=-1.0).then_inc(s_eo, 1)
                    act.wait_ge(s_eo, k + 1)
                    nc.scalar.activation(a, a, ACT.Ln, bias=1.0).then_inc(s_lo1, 1)

        @block.vector
        def _(dve):
            chain = [0]

            def link(ins):
                chain[0] += 1
                ins.then_inc(s_chain, 1)
                dve.wait_ge(s_chain, chain[0])

            V = nc.vector
            V.memset(ones[:, :], 1.0)
            V.memset(attrT[64:96, :, :], 1.0).then_inc(s_ones, 1)
            V.memset(ones_bf[:, :], 1.0)
            dve.wait_ge(s_iota, 2)
            V.tensor_scalar(ident[:, :], column_no[:, :], row_no[:, 0:1], None, ALU.is_equal)
            V.tensor_scalar(earlier[:, :], column_no[:, :], row_no[:, 0:1], None, ALU.is_lt)
            for k in range(3):
                V.tensor_scalar(is_row[:, k:k + 1], row_no[:, 0:1], float(k), None, ALU.is_equal)
            V.tensor_scalar(spare_row[:, :], row_no[:, 0:1], float(N), None, ALU.add).then_inc(s_const, 1)
            dve.wait_ge(s_const, 1)

            link(V.memset(meanvar[:, :, :], 0.0))
            for k, blocks in enumerate(x_pieces):
                dve.wait_ge(s_xs[k], 32 if k == 3 and NLAST < P else 16)
                for b in blocks:
                    r = P if b < NB - 1 else NLAST
                    last = V.bn_stats(stats[0:r, b, :], xs[0:r, b, :])
            link(last)
            dve.wait_ge(s_w, 16 * (7 + 2 * T))
            V.tensor_scalar(bo1_negative[:, :], bo1[:, :], -1.0, None, ALU.mult)
            V.tensor_scalar(bo1_less_ln2[:, :], ones[:, :], bo1[:, 0:1], -LN2, ALU.mult, ALU.add).then_inc(s_shift, 1)
            for b in range(NB):
                r = P if b < NB - 1 else NLAST
                last = V.bn_aggr(meanvar[0:r, b, :], stats[0:r, b, :])
            link(last)
            V.tensor_scalar(std[:, :], meanvar[:, :, 1], 1e-5, None, ALU.add).then_inc(s_var, 1)

            dve.wait_ge(s_w, 16 * (7 + 2 * T))
            dve.wait_ge(s_bias, 1)
            V.tensor_tensor(bo2_row[:, :], ps[6][:, F:2 * F], bo2_row[:, :], ALU.add)
            link(V.scalar_tensor_tensor(bf2_row[:, :], ps[6][:, 0:F], -LN2, bf2_row[:, :], ALU.mult, ALU.add))
            link(V.tensor_copy(bf2_hi[:, :], bf2_row[:, :]))
            link(V.tensor_tensor(bf2_rest[:, :], bf2_row[:, :], bf2_hi[:, :], ALU.subtract))
            link(V.tensor_copy(bf2_mid[:, :], bf2_rest[:, :]))
            V.tensor_scalar(bf2_sum[:, :], bf2_hi[:, :], is_row[:, 0:1], None, ALU.mult)
            link(V.tensor_tensor(bf2_rest[:, :], bf2_rest[:, :], bf2_mid[:, :], ALU.subtract))
            link(V.scalar_tensor_tensor(bf2_sum[:, :], bf2_mid[:, :], is_row[:, 1:2], bf2_sum[:, :], ALU.mult, ALU.add))
            for t in range(T):
                last = V.scalar_tensor_tensor(bf2_parts[:, t, :], bf2_rest[:, :], is_row[:, 2:3], bf2_sum[:, :], ALU.mult, ALU.add)
            last.then_inc(s_biasr, 1)

            dve.wait_ge(s_std, 1)
            link(V.reciprocal(rstd[:, :], std[:, :]))

            def normalize(q):
                for b in quad(q)[0]:
                    r = P if b < NB - 1 else NLAST
                    last = V.tensor_scalar(normed[0:r, b, :], xs[0:r, b, :], meanvar[0:r, b, 0:1], rstd[0:r, b:b + 1],
                                           ALU.subtract, ALU.mult)
                last.then_inc(s_norm, 1)

            def rest_of(q):
                blocks, last = quad(q)
                n = len(blocks)
                r = P if n > 1 else last
                dve.wait_ge(s_hi, q + 1)
                if q >= 3:
                    after_low(dve, q - 3)
                V.tensor_tensor(rest[0:r, q % 3, 0:n * F].rearrange("p (b f) -> p b f", f=F),
                                ps[2 + q % 2][0:r, 0:n * F].rearrange("p (b f) -> p b f", f=F),
                                parts[0:r, q % 4, 0:n, 0, :], ALU.subtract).then_inc(s_rest, 1)

            def extremes(groups):
                if not groups:
                    return
                dve.wait_ge(s_chf, groups[-1] + 1)
                for g in groups:
                    r = rows_of[g]
                    V.tensor_reduce(dst_min[0:r, g:g + 1], chunk_f[0:r, 1, g, :], AX.X, ALU.min)
                    last = V.tensor_reduce(dst_max[0:r, g:g + 1], chunk_f[0:r, 1, g, :], AX.X, ALU.max)
                link(last)

            def diagonals():
                for g in range(G):
                    last = V.tensor_scalar(dst_min[0:rows_of[g], g:g + 1], dst_min[0:rows_of[g], g:g + 1], float(N - P), None, ALU.min)
                link(last)
                for g in range(G):
                    r = rows_of[g]
                    last = V.tensor_tensor(spread[0:r, g:g + 1], dst_max[0:r, g:g + 1], dst_min[0:r, g:g + 1], ALU.subtract)
                link(last)
                for g in range(G):
                    r = rows_of[g]
                    V.tensor_scalar(diag[0:r, g, 0, 0:r], ident[0:r, 0:r], dst_min[0:r, g:g + 1], None, ALU.mult)
                    last = V.tensor_scalar(diag[0:r, g, 1, 0:r], ident[0:r, 0:r], spread[0:r, g:g + 1], None, ALU.mult)
                last.then_inc(s_diag, 1)

            def order():
                dve.wait_ge(s_bps, 1)
                V.tensor_scalar(window_col[:, 0:NCH], ps[6][:, 0:NCH], row_no[:, 0:1], None, ALU.add)
                V.tensor_copy(base_row[0:1, 0:NCH], ps[6][0:1, 0:NCH]).then_inc(s_base, 1)
                link(V.tensor_reduce(widest[0:1, 0:1], ps[7][0:1, 0:NCH], AX.X, ALU.max))
                V.tensor_scalar(in_order[0:1, 0:1], widest[0:1, 0:1], float(P), None, ALU.is_lt).then_inc(s_flag, 1)

            normalize(0)
            if NQ > 1:
                normalize(1)
            for q in range(NQ + 2):
                if q >= 2 and not low_on_gpsimd(q - 2):
                    low(q - 2, dve, s_lo)
                if q + 2 < NQ:
                    normalize(q + 2)
                if q == 0:
                    extremes(range(0, (G + 1) // 2))
                if q == min(1, NQ):
                    extremes(range((G + 1) // 2, G))
                if q == min(2, NQ):
                    diagonals()
                if q == min(6, NQ + 1):
                    order()
                if q < NQ:
                    rest_of(q)

            dve.wait_ge(s_col, 3 * G)
            if REPEATED:
                V.memset(cut_col[0:REPEATED // T, NCH - 1, :], 0.0).then_inc(s_cut, 1)

            def work(in_order):
                def step(i, m):
                    c, slot, odd = i + 1, (m + 1) % 4, (m + 1) % 2
                    if in_order and exists(c):
                        after_slot(dve, s_dstb, c, slot)
                        after(dve, s_xgp, c - 2)
                        V.tensor_scalar(onehot[:, odd, :], dst_b[:, slot, :], window_col[:, bass.ds(c, 1)], None,
                                        ALU.is_equal).then_inc(s_oh, 1)
                    if not in_order and exists(c):
                        after_slot(dve, s_gath, c - 4, slot, T)
                        V.tensor_copy(dst_now[:, slot, :], dst_col[:, bass.ds(c, 1), :].rearrange("p o t -> p (o t)")).then_inc(s_dnow, 1)
                    if exists(i + 1):
                        after(dve, s_log, i + 1)
                        after(dve, s_fp, i - 1)
                        V.scalar_tensor_tensor(hidden[:, (m + 1) % 2, :], hidden_ps[:, :], 0.0, hidden_exp[:, (m + 1) % 2, :],
                                               ALU.max, ALU.add).then_inc(s_h, 1)
                    c, slot, odd = i, m, m % 2
                    if exists(c):
                        after_slot(dve, s_srcb, c, slot)
                        after(dve, s_sp, c - 2)
                        V.tensor_tensor(same[:, odd, :].rearrange("p (t e) -> p t e", t=T),
                                        src_b[:, slot, :].rearrange("p (t e) -> p t e", t=T),
                                        src_col[:, bass.ds(c, 1), :].rearrange("p o t -> p (o t)").unsqueeze(2).to_broadcast([P, T, P]),
                                        ALU.is_equal).then_inc(s_same, 1)
                        for t in range(T):
                            last = V.scalar_tensor_tensor(same_earlier[:, odd, t * P:(t + 1) * P], src_b[:, slot, t * P:(t + 1) * P],
                                                          src_col[:, bass.ds(c, 1), t], earlier[:, :],
                                                          ALU.is_equal, ALU.mult, accum_out=n_earlier[:, slot, t:t + 1])
                        last.then_inc(s_first, 1)
                        if not in_order:
                            after_slot(dve, s_gath, c, slot, T)
                            after(dve, s_xg, c - 2)
                            g = gathered[:, slot, :, :]
                            V.tensor_tensor(two_parts, g[:, :, 0:F], g[:, :, F:2 * F], ALU.add).then_inc(s_two, 1)
                            after(dve, s_two, c)
                            V.tensor_tensor(xg_ps[odd][:, :].rearrange("p (t f) -> p t f", t=T), two_parts,
                                            g[:, :, 2 * F:3 * F], ALU.add).then_inc(s_xgp, 1)
                        after(dve, s_fp, c)
                        after(dve, s_xg, c)
                        V.tensor_tensor(message[:, odd, :], filter_ps[odd][:, :], xg[:, odd, :], ALU.mult).then_inc(s_msg, 1)
                        after(dve, s_first, c)
                        if known(c) and c == 0:
                            dve.wait_ge(s_less, 1)
                        V.scalar_tensor_tensor(picked[:, slot, :], n_earlier[:, slot, :], 0.0,
                                               src_less_spare[:, bass.ds(c, 1), :].rearrange("p o t -> p (o t)"),
                                               ALU.is_equal, ALU.mult).then_inc(s_pick, 1)
                        after(dve, s_pick, c)
                        for t in range(T):
                            after(dve, s_scat[t], c - 4, 16)
                        V.tensor_scalar(target[:, slot, :], picked[:, slot, :], spare_row[:, 0:1], None,
                                        ALU.add).then_inc(s_idx, 1)
                steps(dve, step)
            both_orders(dve, lambda: dve.value_load(in_order[0:1, 0:1], min_val=0, max_val=1), work)

            V.tensor_tensor(xs[:, 0:NB - 1, :], xs[:, 0:NB - 1, :],
                            bo2_row[:, :].unsqueeze(1).to_broadcast([P, NB - 1, F]), ALU.add)
            V.tensor_tensor(xs[0:NLAST, NB - 1, :], xs[0:NLAST, NB - 1, :], bo2_row[0:NLAST, :], ALU.add).then_inc(s_res, 1)
            dve.wait_ge(s_res, 1)

            def add_up(q):
                n, h = len(piece(q)) * F, q % 4
                dve.wait_ge(s_ald[h], 16 * T * (q // 4 + 1))
                V.tensor_tensor(acc_sb[:, h, 0, 0:n], acc_sb[:, h, 0, 0:n], acc_sb[:, h, 1, 0:n], ALU.add).then_inc(s_add01, 1)
                dve.wait_ge(s_add01, q + 1)
                dve.wait_ge(s_add23, q + 1)
                if q >= 2:
                    dve.wait_ge(s_tp, q - 1)
                V.tensor_tensor(total[:, q % 2, 0:n], acc_sb[:, h, 0, 0:n], acc_sb[:, h, 2, 0:n], ALU.add).then_inc(s_add, 1)

            def out_hidden(q):
                n, h = len(piece(q)) * P, q % 2
                dve.wait_ge(s_lo1, q + 1)
                if q >= 2:
                    dve.wait_ge(s_o2, q - 1)
                V.scalar_tensor_tensor(hid_o[:, h, 0:n], ps[4 + h][:, 0:n], bo1_negative[:, 0:1], log_o[:, h, 0:n], ALU.max, ALU.add).then_inc(s_o1s, 1)

            def finish(q):
                b, h = piece(q), q % 2
                r = NLAST if b[-1] == NB - 1 else P
                dve.wait_ge(s_o2, q + 1)
                if q >= 2:
                    dve.wait_ge(s_ost[h], 16 * stores_until(q - 1, h))
                V.tensor_tensor(out_sb[0:r, h, 0:len(b), :], ps[6 + h][0:r, 0:len(b) * F].rearrange("p (b f) -> p b f", f=F),
                                xs[0:r, b[0]:b[-1] + 1, :], ALU.add).then_inc(s_o, 1)

            for q in range(NPC + 3):
                if q < NPC:
                    add_up(q)
                if 2 <= q < NPC + 2:
                    out_hidden(q - 2)
                if q >= 3:
                    finish(q - 3)

        @block.tensor
        def _(pe):
            MM, TR = nc.tensor.matmul, nc.tensor.transpose
            pe.wait_ge(s_const, 1)

            def tr(q):
                blocks, last = quad(q)
                pe.wait_ge(s_norm, q + 1)
                if q >= 2:
                    pe.wait_ge(s_hT, q - 1)
                for j, b in enumerate(blocks):
                    r = last if j == len(blocks) - 1 else P
                    ins = TR(ps[q % 2][:, j * P:j * P + r], normed[0:r, b, :], ident[0:r, 0:r])
                ins.then_inc(s_tr, 1)

            def product(q):
                blocks, last = quad(q)
                pe.wait_ge(s_hT, q + 1)
                if q >= 2:
                    pe.wait_ge(s_rest, q - 1)
                for j, b in enumerate(blocks):
                    r = last if j == len(blocks) - 1 else P
                    ins = MM(ps[2 + q % 2][0:r, j * F:(j + 1) * F], hT[:, q % 2, j * P:j * P + r], w_in[:, :], start=True, stop=True)
                ins.then_inc(s_xw, 1)

            def column(j):
                n, g = divmod(j, G)
                k, r = (1, 2, 0)[n], rows_of[g]
                if k == 2:
                    pe.wait_ge(s_chunks[2], 16 * ndma)
                else:
                    pe.wait_ge(s_chf, (1 - k) * G + g + 1)
                if j >= 2:
                    pe.wait_ge(s_col, j - 1)
                for t in range(T):
                    ins = TR(ps[4 + j % 2][:, t * r:(t + 1) * r],
                             chunk_f[0:r, k, g, :].rearrange("c (p t) -> c t p", t=T)[:, t, :], ident[0:r, 0:r])
                ins.then_inc(s_colps, 1)

            def bases():
                pe.wait_ge(s_diag, 1)
                pe.wait_ge(s_biasr, 1)
                for k in range(2):
                    for g in range(G):
                        r = rows_of[g]
                        ins = MM(ps[6 + k][:, g * P:g * P + r], ones[0:r, :], diag[0:r, g, k, 0:r], start=True, stop=True)
                ins.then_inc(s_bps, 1)

            for j in range(G):
                column(j)
            pe.wait_ge(s_w, 16 * (7 + 2 * T))
            pe.wait_ge(s_shift, 1)
            MM(ps[6][:, 0:F], ones[:, :], w_f2[:, :], start=True, stop=True)
            MM(ps[6][:, F:2 * F], bo1_less_ln2[:, :], w_o2[:, :], start=True, stop=True).then_inc(s_bias, 1)
            for j in range(G, 2 * G):
                column(j)
            for q in range(NQ + 1):
                if q < NQ:
                    tr(q)
                if q >= 1:
                    product(q - 1)
                    if q == min(4, NQ):
                        bases()
                    if 4 <= q < G + 4:
                        column(2 * G + q - 4)
            for q in range(max(NQ + 1, 4), G + 4):
                column(2 * G + q - 4)

            def products(in_order):
                def step(i, m):
                    c, slot, odd = i + 2, (m + 2) % 4, m % 2
                    if exists(c):
                        after_slot(pe, s_attr, c, slot)
                        after(pe, s_aT, c - 1)
                        TR(attrT_ps[0:KA, odd * P:odd * P + P], attr[:, slot, :], ident[:, :]).then_inc(s_aTp, 1)
                    c, odd = i + 1, (m + 1) % 2
                    if exists(c):
                        after(pe, s_aT, c)
                        after(pe, s_h, c - 1)
                        for t in range(T):
                            ins = MM(hidden_ps[:, t * P:(t + 1) * P], w_f1[:, t, :], attrT[0:KA + 1, odd, :], start=True, stop=True)
                        ins.then_inc(s_hp, 1)
                    c, slot, odd = i, m, m % 2
                    if in_order and exists(c):
                        after(pe, s_oh, c)
                        after_slot(pe, s_xwin, c, slot)
                        after(pe, s_xg, c - 2)
                        for t in range(T):
                            for k in range(3):
                                ins = MM(xg_ps[odd][:, t * F:(t + 1) * F], onehot[:, odd, t * P:(t + 1) * P],
                                         xwin[:, slot, k * F:(k + 1) * F], start=(k == 0), stop=(k == 2))
                        ins.then_inc(s_xgp, 1)
                    if exists(c):
                        after(pe, s_h, c)
                        after(pe, s_msg, c - 2)
                        MM(filter_ps[odd][:, :], ones_bf[:, :], bf2_parts[:, :, :].rearrange("p t f -> p (t f)"),
                           start=True, stop=False, skip_group_check=True)
                        for t in range(T):
                            ins = MM(filter_ps[odd][:, t * F:(t + 1) * F], hidden[:, odd, t * P:(t + 1) * P], w_f2[:, :],
                                     start=False, stop=(t == T - 1), skip_group_check=True)
                        ins.then_inc(s_fp, 1)
                    c, odd = i - 1, (m - 1) % 2
                    if exists(c):
                        after(pe, s_same, c)
                        after(pe, s_msg, c)
                        after(pe, s_s, c - 2)
                        for t in range(T):
                            ins = MM(summed_ps[odd][:, t * F:(t + 1) * F], same[:, odd, t * P:(t + 1) * P],
                                     message[:, odd, t * F:(t + 1) * F], start=True, stop=True)
                        ins.then_inc(s_sp, 1)
                steps(pe, step)
            both_orders(pe, lambda: pe.value_load(in_order[0:1, 0:1], min_val=0, max_val=1), products)

            for q in range(NPC + 2):
                if q < NPC:
                    n, h = len(piece(q)), q % 2
                    pe.wait_ge(s_add, q + 1)
                    if q >= 2:
                        pe.wait_ge(s_t, q - 1)
                    for j in range(n):
                        ins = TR(ps[2 + h][:, j * P:(j + 1) * P], total[:, h, j * F:(j + 1) * F], ident[:, :])
                    ins.then_inc(s_tp, 1)
                if 1 <= q < NPC + 1:
                    k, h = q - 1, (q - 1) % 2
                    n = len(piece(k)) * P
                    pe.wait_ge(s_t, k + 1)
                    if k >= 2:
                        pe.wait_ge(s_o1s, k - 1)
                    MM(ps[4 + h][:, 0:n], w_o1[:, :], totalT[:, h, 0:n], start=True, stop=True).then_inc(s_o1, 1)
                if q >= 2:
                    k, h = q - 2, q % 2
                    pe.wait_ge(s_o1s, k + 1)
                    if k >= 2:
                        pe.wait_ge(s_o, k - 1)
                    for j in range(len(piece(k))):
                        ins = MM(ps[6 + h][:, j * F:(j + 1) * F], hid_o[:, h, j * P:(j + 1) * P], w_o2[:, :], start=True, stop=True)
                    ins.then_inc(s_o2, 1)


_INS = ['x', 'src', 'dst', 'edge_attr_20', 'edge_weight1', 'L0_gnn_W_in', 'L0_gnn_W_f1', 'L0_gnn_b_f1', 'L0_gnn_W_f2',
        'L0_gnn_b_f2', 'L0_gnn_W_o1', 'L0_gnn_b_o1', 'L0_gnn_W_o2', 'L0_gnn_b_o2']


def kernel(**inputs):
    import numpy as _np
    import concourse.bacc as _bacc
    from concourse import mybir as _mybir
    from concourse.bass_utils import run_bass_kernel_spmd as _run

    nc = _bacc.Bacc("TRN2", target_bir_lowering=False, num_devices=1)
    arrays, args = {}, []
    for name in _INS:
        a = _np.ascontiguousarray(inputs[name])
        arrays[f"in_{name}_dram"] = a
        args.append(nc.dram_tensor(f"in_{name}_dram", a.shape, _mybir.dt.from_np(a.dtype), kind="ExternalInput").ap())
    shape = arrays["in_x_dram"].shape
    args.append(nc.dram_tensor("out_dram", shape, _mybir.dt.float32, kind="ExternalOutput").ap())
    gnn_kernel(nc, *args)
    r = _run(nc, [arrays], core_ids=[0])
    return r.results[0]["out_dram"]
```
